# Optimizing a Trainium2 kernel written in Bass

```python
import numpy as np
import jax
import jax.numpy as jnp

def _softmax(x, axis=-1):
    return jax.nn.softmax(x, axis=axis)
def _gelu(x):
    return jax.nn.gelu(x, approximate=True)
def _silu(x):
    return jax.nn.silu(x)
def _sigmoid(x):
    return jax.nn.sigmoid(x)
def _layernorm(x, axis=-1, eps=1e-5):
    m = jnp.mean(x, axis=axis, keepdims=True)
    v = jnp.var(x, axis=axis, keepdims=True)
    return (x - m) / jnp.sqrt(v + eps)
def _scatter_add(tgt, idx, src, axis=0):
    return tgt.at[idx].add(src)
def _segment_sum(src, seg, n):
    return jax.ops.segment_sum(src, seg, n)

kernel_name = 'mk_conv_preact_d2_conv_nchw512_8159a9'

def setup_inputs(seed: int = 0):
    np.random.seed(seed)
    _w = jnp.asarray
    def _rec_inputs():
        import jax
        import jax.numpy as jnp
        _gk = jax.random.key(seed)
        x = -0.0005207 + 1.001 * jax.random.normal(jax.random.fold_in(_gk, 1), (1, 512, 64, 64), jnp.float32)
        return x
    x = _rec_inputs()
    def _L0_conv_setup():
        import jax, jax.numpy as jnp
        import numpy as np
        HEADS = 8

        def _conv1x1(x, w, gain):
            return jnp.einsum('bcxy,oc->boxy', x, w * gain)
        key = jax.random.key(seed)
        ks = jax.random.split(key, 5)
        B, C, H, W = (1, 512, 64, 64)
        dim_inner = 512
        fmap = jax.random.normal(ks[0], (B, C, H, W), jnp.float32)
        wq = jax.random.normal(ks[1], (dim_inner, C), jnp.float32)
        wk = jax.random.normal(ks[2], (dim_inner, C), jnp.float32)
        wv = jax.random.normal(ks[3], (dim_inner, C), jnp.float32)
        wo = jax.random.normal(ks[4], (C, dim_inner), jnp.float32)
        return {'fmap': fmap, 'wq': wq, 'wk': wk, 'wv': wv, 'wo': wo}
    _L0_conv_all = _L0_conv_setup()
    _L0_conv_in = {k: v for k, v in _L0_conv_all.items() if k in ('wq', 'wk', 'wv', 'wo', )}
    del _L0_conv_all

    def _L1_conv_setup():
        import jax, jax.numpy as jnp
        import numpy as np
        SCOPE = 63
        IN_CHANNELS = 512
        DAMP = 0.12
        STD = 8.0

        def _mexican_hat(scope, damping, std):
            x = jnp.arange(scope, dtype=jnp.float32) - (scope - 1) / 2.0
            norm = damping * (2.0 / (jnp.sqrt(3.0 * std) * np.pi ** 0.25))
            k = norm * (1.0 - (x / std) ** 2) * jnp.exp(-x ** 2 / (2.0 * std ** 2))
            return k[None, None, :]

        def _pad_roll(k, in_channels, scope):
            pad_left = (in_channels - scope) // 2
            pad_right = in_channels - scope - pad_left
            padded = jnp.concatenate([jnp.zeros((pad_left,), k.dtype), k, jnp.zeros((pad_right,), k.dtype)])
            return jnp.roll(padded, in_channels // 2 + 1)
        key = jax.random.key(seed)
        activations = jax.random.normal(key, (32, IN_CHANNELS, 56, 56), dtype=jnp.float32)
        inhibition_filter = _mexican_hat(SCOPE, DAMP, STD)
        return {'activations': activations, 'inhibition_filter': inhibition_filter}
    _L1_conv_all = _L1_conv_setup()
    _L1_conv_in = {k: v for k, v in _L1_conv_all.items() if k in ('inhibition_filter', )}
    del _L1_conv_all

    return {
        "x": x,
        "L0_conv_wq": _L0_conv_in["wq"],
        "L0_conv_wk": _L0_conv_in["wk"],
        "L0_conv_wv": _L0_conv_in["wv"],
        "L0_conv_wo": _L0_conv_in["wo"],
        "L1_conv_inhibition_filter": _L1_conv_in["inhibition_filter"],
    }

def reference(x, L0_conv_wq, L0_conv_wk, L0_conv_wv, L0_conv_wo, L1_conv_inhibition_filter):
    import jax
    import jax.numpy as jnp
    def _L0_conv_ref(fmap, wq, wk, wv, wo):
        import jax, jax.numpy as jnp
        import numpy as np
        HEADS = 8

        def _conv1x1(x, w, gain):
            return jnp.einsum('bcxy,oc->boxy', x, w * gain)
        B, C, H, W = fmap.shape
        h = HEADS
        dim_inner = wq.shape[0]
        d = dim_inner // h
        scale = d ** (-0.5)
        gain_in = 1.0 / np.sqrt(C)
        gain_out = 1.0 / np.sqrt(dim_inner)

        def to_tokens(t):
            return t.reshape(B, h, d, H * W).transpose(0, 1, 3, 2).reshape(B * h, H * W, d)
        q = to_tokens(_conv1x1(fmap, wq, gain_in))
        k = to_tokens(_conv1x1(fmap, wk, gain_in))
        v = to_tokens(_conv1x1(fmap, wv, gain_in))
        AA = jnp.sum(q * q, axis=-1)
        qk = jnp.einsum('bid,bjd->bij', q, k)
        sim = -(AA[:, :, None] + AA[:, None, :] - 2.0 * qk) * scale
        attn = jax.nn.softmax(sim, axis=-1)
        out = jnp.einsum('bij,bjd->bid', attn, v)
        out = out.reshape(B, h, H, W, d).transpose(0, 1, 4, 2, 3).reshape(B, h * d, H, W)
        return _conv1x1(out, wo, gain_out)

    def _L1_conv_ref(activations, inhibition_filter):
        import jax, jax.numpy as jnp
        import numpy as np
        SCOPE = 63
        IN_CHANNELS = 512
        DAMP = 0.12
        STD = 8.0

        def _mexican_hat(scope, damping, std):
            x = jnp.arange(scope, dtype=jnp.float32) - (scope - 1) / 2.0
            norm = damping * (2.0 / (jnp.sqrt(3.0 * std) * np.pi ** 0.25))
            k = norm * (1.0 - (x / std) ** 2) * jnp.exp(-x ** 2 / (2.0 * std ** 2))
            return k[None, None, :]

        def _pad_roll(k, in_channels, scope):
            pad_left = (in_channels - scope) // 2
            pad_right = in_channels - scope - pad_left
            padded = jnp.concatenate([jnp.zeros((pad_left,), k.dtype), k, jnp.zeros((pad_right,), k.dtype)])
            return jnp.roll(padded, in_channels // 2 + 1)
        C = activations.shape[1]
        kernel = _pad_roll(inhibition_filter[0, 0], C, SCOPE)
        idx = (jnp.arange(C)[None, :] - jnp.arange(C)[:, None]) % C
        tpl = kernel[idx]
        return jnp.einsum('bchw,cd->bdhw', activations, tpl)

    def _gn(v, G=32, eps=1e-5):
        B_, C_, H_, W_ = v.shape
        g = v.reshape(B_, G, C_ // G, H_, W_)
        m = jnp.mean(g, axis=(2, 3, 4), keepdims=True)
        s = jnp.var(g, axis=(2, 3, 4), keepdims=True)
        return ((g - m) / jnp.sqrt(s + eps)).reshape(v.shape)

    def _ln_c(v, eps=1e-6):
        m = jnp.mean(v, axis=1, keepdims=True)
        s = jnp.var(v, axis=1, keepdims=True)
        return (v - m) / jnp.sqrt(s + eps)

    def _ln_t(v, eps=1e-5):
        m = jnp.mean(v, axis=-1, keepdims=True)
        s = jnp.var(v, axis=-1, keepdims=True)
        return (v - m) / jnp.sqrt(s + eps)

    def _to_tokens(v):
        B_, C_, H_, W_ = v.shape
        return v.reshape(B_, C_, H_ * W_).transpose(0, 2, 1)
    def _from_tokens(t, like):
        B_, C_, H_, W_ = like.shape
        return t.transpose(0, 2, 1).reshape(B_, C_, H_, W_)

    x = x + _L0_conv_ref(_gn(x), L0_conv_wq, L0_conv_wk, L0_conv_wv, L0_conv_wo)
    x = x + _L1_conv_ref(_gn(x), L1_conv_inhibition_filter)
    return x


_drawn_inputs = setup_inputs


def setup_inputs(seed=0):
    import zlib

    import numpy as np

    out = dict(_drawn_inputs(seed))
    spreads = {}
    factors = {}
    for name, (base, spread) in spreads.items():
        noise = np.random.default_rng([zlib.crc32(name.encode()), seed]).standard_normal(out[name].shape)
        drawn = base * np.exp(spread * noise) if base else spread * noise
        out[name] = jnp.asarray(drawn.astype(out[name].dtype))
    for name, factor in factors.items():
        out[name] = (out[name] * factor).astype(out[name].dtype)
    return out
```

```python
from contextlib import ExitStack

import concourse.bass as bass
from concourse import mybir

F32 = mybir.dt.float32
F32R = mybir.dt.float32r
ALU = mybir.AluOpType
ACT = mybir.ActivationFunctionType
AX = mybir.AxisListType

C = 512
N = 4096
HEADS = 8
D = C // HEADS
P = 128
CT = C // P
CH = 512
NCH = N // CH
GAIN = float(C) ** -0.5
SCOPE = 63
GN_EPS = 1e-5

TILES = (HEADS // 2) * NCH
JT = N // P
UNITS = 2 * (CH // P) * NCH
UNITS_PER_STEP = 5
PSLOTS = 8
POOL_SLOTS = (1, 2, 3, 5, 6, 7)
DVE_JTS = [j for j in range(JT) if j % PSLOTS not in POOL_SLOTS]
POOL_JTS = [j for j in range(JT) if j % PSLOTS in POOL_SLOTS]
DVE_OPS = len(DVE_JTS) - 1
POOL_OPS = len(POOL_JTS) - 1
KM_DMAS, KAB_DMAS, QM_DMAS, QAB_DMAS = 4, 7, 2, 6


def group_statistics(nc, block, sem, engines, stats, mv, ex, psum, gmat, root, mean, rstd, ready):
    step = sem("gn_step")
    sums = sem("gn_sums")
    rooted = sem("gn_root")

    def vector(dve):
        for m in range(CT):
            nc.vector.bn_aggr(mv[:, m, :], stats[:, m, :, :]).then_inc(step, 1)
        dve.wait_ge(step, CT)
        nc.vector.tensor_tensor(ex[:, :, 0], mv[:, :, 0], mv[:, :, 0], ALU.mult).then_inc(step, 1)
        dve.wait_ge(step, CT + 1)
        nc.vector.tensor_tensor(mv[:, :, 1], mv[:, :, 1], ex[:, :, 0], ALU.add).then_inc(step, 1)
        dve.wait_ge(sums, 1)
        nc.vector.tensor_copy(mean[:, :], psum[:, :, 0]).then_inc(step, 1)
        dve.wait_ge(step, CT + 3)
        nc.vector.tensor_tensor(ex[:, :, 0], mean[:, :], mean[:, :], ALU.mult).then_inc(step, 1)
        dve.wait_ge(step, CT + 4)
        nc.vector.tensor_tensor(ex[:, :, 1], psum[:, :, 1], ex[:, :, 0], ALU.subtract).then_inc(step, 1)
        dve.wait_ge(step, CT + 5)
        nc.vector.tensor_scalar(root[:, :, 0], ex[:, :, 1], GN_EPS, None, ALU.add).then_inc(step, 1)
        dve.wait_ge(rooted, 1)
        nc.vector.reciprocal(ex[:, :, 0], root[:, :, 1]).then_inc(step, 1)
        dve.wait_ge(step, CT + 7)
        nc.vector.tensor_tensor(ex[:, :, 1], root[:, :, 0], ex[:, :, 0], ALU.mult).then_inc(step, 1)
        dve.wait_ge(step, CT + 8)
        nc.vector.tensor_tensor(ex[:, :, 0], ex[:, :, 1], root[:, :, 1], ALU.add).then_inc(step, 1)
        dve.wait_ge(step, CT + 9)
        nc.vector.tensor_scalar(ex[:, :, 1], ex[:, :, 0], 0.5, None, ALU.mult).then_inc(step, 1)
        dve.wait_ge(step, CT + 10)
        nc.vector.reciprocal(rstd[:, :], ex[:, :, 1]).then_inc(ready, 1)
        dve.wait_ge(ready, 1)

    def tensor(pe):
        pe.wait_ge(step, CT + 2)
        nc.tensor.matmul(psum[:, :, :].rearrange("p m s -> p (m s)"), gmat[:, :],
                         mv[:, :, :].rearrange("p m s -> p (m s)"), start=True, stop=True).then_inc(sums, 1)

    def scalar(act):
        act.wait_ge(step, CT + 6)
        nc.scalar.activation(root[:, :, 1], root[:, :, 0], ACT.Sqrt).then_inc(rooted, 1)

    return vector, tensor, scalar


def projections(nc, x, wq_t, wk_t, wv_t, gmat_d, sel_d, q_s, k_s, v_s, aa_s):
    with ExitStack() as ctx:
        def sb(name, shape, dt=F32):
            return ctx.enter_context(nc.sbuf_tensor(name, shape, dt))

        def sem(name):
            return ctx.enter_context(nc.semaphore(name))

        x_sb = sb("p1_x", [P, CT, N])
        w_hi = sb("p1_w_hi", [P, 3, CT, C], F32R)
        w_lo = sb("p1_w_lo", [P, 3, CT, C], F32R)
        raw = sb("p1_raw", [P, CT, CH])
        xn_hi = sb("p1_xn_hi", [P, 2, CT, CH], F32R)
        xn_lo = sb("p1_xn_lo", [P, 2, CT, CH], F32R)
        qk_st = sb("p1_qk_st", [P, 2, 2, CH], F32R)
        v_st = sb("p1_v_st", [P, 2, CH])
        sq = sb("p1_sq", [P, 2, CH])
        aa_st = sb("p1_aa_st", [2, 2, 2, CH], F32R)
        gmat = sb("p1_gmat", [P, P])
        sel = sb("p1_sel", [P, 2])
        stats = sb("p1_stats", [P, CT, NCH, 6])
        mv = sb("p1_mv", [P, CT, 2])
        ex = sb("p1_ex", [P, CT, 2])
        root = sb("p1_root", [P, CT, 2])
        mean = sb("p1_mean", [P, CT])
        rstd = sb("p1_rstd", [P, CT])
        acc = ctx.enter_context(nc.psum_tensor("p1_acc", [P, 4, CH], F32))
        aa_ps = ctx.enter_context(nc.psum_tensor("p1_aa", [P, 2, CH], F32))
        gn_ps = ctx.enter_context(nc.psum_tensor("p1_gn", [P, CT, 2], F32))

        x_loaded = [sem(f"p1_x_loaded{m}") for m in range(CT)]
        consts_loaded = sem("p1_consts_loaded")
        w_loaded = sem("p1_w_loaded")
        w_hi_done = sem("p1_w_hi_done")
        w_lo_done = sem("p1_w_lo_done")
        stats_done = sem("p1_stats_done")
        gn_ready = sem("p1_gn_ready")
        xn_done = sem("p1_xn_done")
        xn_hi_done = sem("p1_xn_hi_done")
        xn_lo_done = sem("p1_xn_lo_done")
        qk_ready = sem("p1_qk_ready")
        v_ready = sem("p1_v_ready")
        aa_ready = sem("p1_aa_ready")
        qk_hi_done = sem("p1_qk_hi_done")
        qk_lo_done = sem("p1_qk_lo_done")
        sq_done = sem("p1_sq_done")
        v_done = sem("p1_v_done")
        aa_hi_done = sem("p1_aa_hi_done")
        aa_lo_done = sem("p1_aa_lo_done")
        qk_stored = [sem(f"p1_qk_stored{s}") for s in range(2)]
        v_stored = [sem(f"p1_v_stored{s}") for s in range(2)]
        aa_stored = [sem(f"p1_aa_stored{s}") for s in range(2)]
        gn_vector, gn_tensor, gn_scalar = group_statistics(
            nc, None, lambda n: sem("p1_" + n), None, stats, mv, ex, gn_ps, gmat, root, mean, rstd, gn_ready)
        block = ctx.enter_context(nc.Block())
        weights = (wq_t, wk_t, wv_t)

        def wait_bank(pe, n, p, first):
            m, kind = divmod((p - 4) % 12, 3)
            before = n if p >= 4 else n - 1
            if first and p < 4:
                return
            if kind == 2:
                pe.wait_ge(v_done, 4 * before + m + 1)
            else:
                pe.wait_ge(qk_lo_done, 8 * before + 2 * m + kind + 1)

        @block.sync
        def _(sp):
            sp.dma_start(gmat[:, :], gmat_d).then_inc(consts_loaded, 16)
            sp.dma_start(sel[:, :], sel_d).then_inc(consts_loaded, 16)
            for m in range(CT):
                for half in range(2):
                    cols = slice(half * N // 2, (half + 1) * N // 2)
                    sp.dma_start(x_sb[:, m, cols], x[m * P:(m + 1) * P, cols]).then_inc(x_loaded[m], 16)
            with sp.Fori(0, NCH, 1) as n:
                for m in range(CT):
                    for kind, dst in enumerate((q_s, k_s)):
                        sp.wait_ge(qk_lo_done, 8 * n + 2 * m + kind + 1)
                        for h in range(2):
                            sp.dma_start(dst[2 * m + h, :, :, bass.ts(n, CH)].rearrange("s c n -> c s n"),
                                         qk_st[h * D:(h + 1) * D, kind, :, :].bitcast(F32)
                                         ).then_inc(qk_stored[kind], 16)
                    sp.wait_ge(v_done, 4 * n + m + 1)
                    sp.dma_start(v_s[:, :, 4 * n + m, :].rearrange("q p d -> p q d"),
                                 v_st[:, m % 2, :].rearrange("p (q d) -> p q d", q=CT)
                                 ).then_inc(v_stored[m % 2], 16)
                    sp.wait_ge(aa_lo_done, 4 * n + m + 1)
                    sp.dma_start(aa_s[2 * m:2 * m + 2, :, bass.ts(n, CH)],
                                 aa_st[:, m % 2, :, :].bitcast(F32)).then_inc(aa_stored[m % 2], 16)
            for s in range(2):
                sp.wait_ge(qk_stored[s], 32 * CT * NCH)
                sp.wait_ge(v_stored[s], 16 * CT * NCH // 2)
                sp.wait_ge(aa_stored[s], 16 * CT * NCH // 2)

        @block.scalar
        def _(act):
            for w, src in enumerate(weights):
                if w:
                    act.wait_ge(w_lo_done, w)
                act.dma_start(raw[:, :, :], src.rearrange("(m p) o -> p m o", p=P)).then_inc(w_loaded, 16)
                act.wait_ge(w_loaded, 16 * (w + 1))
                nc.scalar.copy(w_hi[:, w, :, :], raw[:, :, :]).then_inc(w_hi_done, 1)
            gn_scalar(act)

            def normalised_hi(n, slot, first=False):
                act.wait_ge(xn_done, CT * (n + 1))
                if not first:
                    act.wait_ge(qk_ready, 8 * (n - 1))
                    act.wait_ge(v_ready, 4 * (n - 1))
                nc.scalar.copy(xn_hi[:, slot, :, :], raw[:, :, :]).then_inc(xn_hi_done, 1)

            def evacuate(n, slot, prepare):
                for m in range(CT):
                    for kind in range(2):
                        p = 3 * m + kind
                        act.wait_ge(qk_ready, 8 * n + 2 * m + kind + 1)
                        act.wait_ge(qk_stored[kind], 32 * (4 * n + m))
                        nc.scalar.mul(qk_st[:, kind, 0, :], acc[:, p % 4, :], GAIN).then_inc(qk_hi_done, 1)
                        if kind == 0:
                            act.wait_ge(aa_ready, 4 * n + max(m - 1, 0))
                            nc.scalar.activation(sq[:, m % 2, :], acc[:, p % 4, :], ACT.Square,
                                                 scale=GAIN).then_inc(sq_done, 1)
                    act.wait_ge(v_ready, 4 * n + m + 1)
                    act.wait_ge(v_stored[m % 2], 16 * (2 * n + m // 2))
                    nc.scalar.mul(v_st[:, m % 2, :], acc[:, (3 * m + 2) % 4, :], GAIN).then_inc(v_done, 1)
                    if m == 1 and prepare:
                        normalised_hi(n + 1, 1 - slot)
                    act.wait_ge(aa_ready, 4 * n + m + 1)
                    act.wait_ge(aa_stored[m % 2], 16 * (2 * n + m // 2))
                    nc.scalar.copy(aa_st[:, m % 2, 0, :], aa_ps[0:2, m % 2, :]).then_inc(aa_hi_done, 1)

            normalised_hi(0, 0, first=True)
            act.wait_ge(xn_lo_done, 1)
            act.wait_ge(xn_done, 2 * CT)
            nc.scalar.copy(xn_hi[:, 1, :, :], raw[:, :, :]).then_inc(xn_hi_done, 1)
            evacuate(0, 0, False)
            with act.Fori(0, (NCH - 2) // 2, 1) as k:
                n = 2 * k + 1
                evacuate(n, 1, True)
                evacuate(n + 1, 0, True)
            evacuate(NCH - 1, 1, False)

        @block.vector
        def _(dve):
            for w in range(len(weights)):
                dve.wait_ge(w_hi_done, w + 1)
                nc.vector.tensor_tensor(w_lo[:, w, :, :], raw[:, :, :], w_hi[:, w, :, :].bitcast(F32),
                                        ALU.subtract).then_inc(w_lo_done, 1)
            for m in range(CT):
                dve.wait_ge(x_loaded[m], 32)
                for k in range(NCH):
                    nc.vector.bn_stats(stats[:, m, k, :], x_sb[:, m, k * CH:(k + 1) * CH]).then_inc(stats_done, 1)
            dve.wait_ge(stats_done, CT * NCH)
            gn_vector(dve)
            dve.wait_ge(w_lo_done, len(weights))

            def normalise(n):
                for m in range(CT):
                    nc.vector.tensor_scalar(raw[:, m, :], x_sb[:, m, bass.ts(n, CH)], mean[:, m:m + 1],
                                            rstd[:, m:m + 1], ALU.subtract, ALU.mult).then_inc(xn_done, 1)

            def normalised_lo(n, slot):
                dve.wait_ge(xn_hi_done, n + 1)
                dve.wait_ge(xn_done, CT * (n + 1))
                nc.vector.tensor_tensor(xn_lo[:, slot, :, :], raw[:, :, :], xn_hi[:, slot, :, :].bitcast(F32),
                                        ALU.subtract).then_inc(xn_lo_done, 1)

            def evacuate(n, slot, prepare):
                for m in range(CT):
                    if m == 0 and prepare:
                        dve.wait_ge(xn_lo_done, n + 1)
                        normalise(n + 1)
                    for kind in range(2):
                        dve.wait_ge(qk_hi_done, 8 * n + 2 * m + kind + 1)
                        if kind == 0:
                            dve.wait_ge(sq_done, 4 * n + m + 1)
                        nc.vector.scalar_tensor_tensor(
                            out=qk_st[:, kind, 1, :], in0=acc[:, (3 * m + kind) % 4, :], scalar=GAIN,
                            in1=qk_st[:, kind, 0, :].bitcast(F32), op0=ALU.mult,
                            op1=ALU.subtract).then_inc(qk_lo_done, 1)
                    if m == 1 and prepare:
                        normalised_lo(n + 1, 1 - slot)
                    dve.wait_ge(aa_hi_done, 4 * n + m + 1)
                    nc.vector.tensor_tensor(aa_st[:, m % 2, 1, :], aa_ps[0:2, m % 2, :],
                                            aa_st[:, m % 2, 0, :].bitcast(F32), ALU.subtract).then_inc(aa_lo_done, 1)

            normalise(0)
            normalised_lo(0, 0)
            dve.wait_ge(xn_lo_done, 1)
            normalise(1)
            normalised_lo(1, 1)
            evacuate(0, 0, False)
            with dve.Fori(0, (NCH - 2) // 2, 1) as k:
                n = 2 * k + 1
                evacuate(n, 1, True)
                evacuate(n + 1, 0, True)
            evacuate(NCH - 1, 1, False)

        @block.tensor
        def _(pe):
            pe.wait_ge(consts_loaded, 32)
            gn_tensor(pe)

            def group(n, slot, p, first):
                m, kind = divmod(p, 3)
                wait_bank(pe, n, p, first)
                cols = slice(m * P, (m + 1) * P)
                for i in range(3 * CT):
                    c, term = divmod(i, 3)
                    if kind == 2:
                        stationary = (xn_lo if term == 2 else xn_hi)[:, slot, c, cols]
                        moving = (w_lo if term == 1 else w_hi)[:, 2, c, :]
                    else:
                        stationary = (w_lo if term == 2 else w_hi)[:, kind, c, cols]
                        moving = (xn_lo if term == 1 else xn_hi)[:, slot, c, :]
                    last = nc.tensor.matmul(acc[:, p % 4, :], stationary, moving,
                                            start=(i == 0), stop=(i == 3 * CT - 1))
                last.then_inc(v_ready if kind == 2 else qk_ready, 1)

            def chunk(n, slot, first=False):
                pe.wait_ge(xn_lo_done, n + 1)
                for m in range(CT):
                    for kind in range(3):
                        group(n, slot, 3 * m + kind, first)
                    pe.wait_ge(sq_done, 4 * n + m + 1)
                    pe.wait_ge(aa_lo_done, 4 * n + max(m - 1, 0))
                    nc.tensor.matmul(aa_ps[0:2, m % 2, :], sel[:, :], sq[:, m % 2, :],
                                     start=True, stop=True).then_inc(aa_ready, 1)

            pe.wait_ge(w_lo_done, len(weights))
            chunk(0, 0, first=True)
            with pe.Fori(0, (NCH - 2) // 2, 1) as k:
                n = 2 * k + 1
                chunk(n, 1)
                chunk(n + 1, 0)
            chunk(NCH - 1, 1)


def attention(nc, ident_d, q_s, k_s, v_s, aa_s, o_s):
    with ExitStack() as ctx:
        def sb(name, shape, dt=F32):
            return ctx.enter_context(nc.sbuf_tensor(name, shape, dt))

        def sem(name):
            return ctx.enter_context(nc.semaphore(name))

        k_max = sb("p2_k_max", [D + 2, 2, N], F32R)
        k_one = sb("p2_k_one", [P, 2, N], F32R)
        k_two = sb("p2_k_two", [D + 3, 2, N], F32R)
        v_sb = sb("p2_v", [P, JT, P])
        q_max = sb("p2_q_max", [D + 2, 2, 2, CH], F32R)
        q_one = sb("p2_q_one", [P, 2, 2, CH], F32R)
        q_two = sb("p2_q_two", [D + 3, 2, 2, CH], F32R)
        probs = sb("p2_probs", [P, PSLOTS, 2, CH])
        row_max = sb("p2_row_max", [P, 2 * CH // P, NCH])
        r_col = sb("p2_r_col", [P, 2 * CH // P])
        r_row = sb("p2_r_row", [2 * CH // P, 2, P], F32R)
        den_dve = sb("p2_den_dve", [P, 2, CH])
        den_pool = sb("p2_den_pool", [P, 2, CH])
        den_sum = sb("p2_den_sum", [P, 2, CH])
        out_raw = sb("p2_out_raw", [P, CH])
        den_inv = sb("p2_den_inv", [P, CH])
        out_norm = sb("p2_out_norm", [P, 2, CH])
        ident = sb("p2_ident", [P, P])
        ones = sb("p2_ones", [P, D])
        scores = ctx.enter_context(nc.psum_tensor("p2_scores", [P, 2, 2, CH], F32))
        max_ps = ctx.enter_context(nc.psum_tensor("p2_max", [P, 2, CH], F32))
        out_ps = ctx.enter_context(nc.psum_tensor("p2_out", [P, CH], F32))
        misc_ps = ctx.enter_context(nc.psum_tensor("p2_misc", [P, CH], F32))

        consts_loaded = sem("p2_consts_loaded")
        q_max_set, q_two_set, k_two_set, ones_set = (
            sem(f"p2_{n}_set") for n in ("q_max", "q_two", "k_two", "ones"))
        km_loaded = [sem(f"p2_km_loaded{c}") for c in range(NCH)]
        kab_loaded = [sem(f"p2_kab_loaded{c}") for c in range(NCH)]
        qm_loaded = [sem(f"p2_qm_loaded{s}") for s in range(2)]
        qab_loaded = [sem(f"p2_qab_loaded{s}") for s in range(2)]
        r_loaded = [sem(f"p2_r_loaded{s}") for s in range(2)]
        max_ready = sem("p2_max_ready")
        max_read = sem("p2_max_read")
        r_ready = sem("p2_r_ready")
        r_turned = sem("p2_r_turned")
        r_copied = sem("p2_r_copied")
        scores_ready = sem("p2_scores_ready")
        probs_ready = sem("p2_probs_ready")
        probs_used = sem("p2_probs_used")
        dve_added = sem("p2_dve_added")
        pool_added = sem("p2_pool_added")
        den_summed = sem("p2_den_summed")
        den_ready = sem("p2_den_ready")
        den_inverted = sem("p2_den_inverted")
        out_copied = sem("p2_out_copied")
        normalised = sem("p2_normalised")
        out_stored = [sem(f"p2_out_stored{s}") for s in range(2)]
        block = ctx.enter_context(nc.Block())

        def dve_ops_through(jt):
            return max(DVE_JTS.index(jt), 1)

        def pool_ops_through(jt):
            return max(POOL_JTS.index(jt), 1)

        def units_of(step):
            return range(min(UNITS_PER_STEP * step, UNITS), min(UNITS_PER_STEP * (step + 1), UNITS))

        @block.sync
        def _(sp):
            sp.dma_start(ident[:, :], ident_d).then_inc(consts_loaded, 16)

            def load_k_max(pair, c):
                for h in range(2):
                    cols = slice(c * CH, (c + 1) * CH)
                    sp.dma_start(k_max[0:D, h, cols].bitcast(F32),
                                 k_s[2 * pair + h, 0, :, cols]).then_inc(km_loaded[c], 16)
                    sp.dma_start(k_max[D:D + 2, h, cols].bitcast(F32),
                                 aa_s[2 * pair + h, :, cols]).then_inc(km_loaded[c], 16)

            def load_k_and_v(pair, c):
                cols = slice(c * CH, (c + 1) * CH)
                for h in range(2):
                    head = 2 * pair + h
                    sp.dma_start(k_one[:, h, cols].bitcast(F32),
                                 k_s[head, :, :, cols].rearrange("s c n -> (s c) n")).then_inc(kab_loaded[c], 16)
                    sp.dma_start(k_two[0:D, h, cols].bitcast(F32), k_s[head, 0, :, cols]).then_inc(kab_loaded[c], 16)
                    sp.dma_start(k_two[D:D + 2, h, cols].bitcast(F32),
                                 aa_s[head, :, cols]).then_inc(kab_loaded[c], 16)
                sp.dma_start(v_sb[:, 4 * c:4 * c + 4, :],
                             v_s[pair, :, 4 * c:4 * c + 4, :]).then_inc(kab_loaded[c], 16)

            def load_q_max(pair, chunk, slot):
                for h in range(2):
                    sp.dma_start(q_max[0:D, slot, h, :].bitcast(F32),
                                 q_s[2 * pair + h, 0, :, bass.ts(chunk, CH)]).then_inc(qm_loaded[slot], 16)

            def load_q(pair, chunk, slot):
                for h in range(2):
                    head, cols = 2 * pair + h, bass.ts(chunk, CH)
                    sp.dma_start(q_one[0:D, slot, h, :].bitcast(F32),
                                 q_s[head, 0, :, cols]).then_inc(qab_loaded[slot], 16)
                    sp.dma_start(q_one[D:P, slot, h, :].bitcast(F32),
                                 q_s[head, 0, :, cols]).then_inc(qab_loaded[slot], 16)
                    sp.dma_start(q_two[0:D, slot, h, :].bitcast(F32),
                                 q_s[head, 1, :, cols]).then_inc(qab_loaded[slot], 16)

            def load_r(tile, slot):
                sp.wait_ge(r_copied, tile + 1)
                for h in range(2):
                    sp.dma_start(q_two[D + 2:D + 3, slot, h, :].rearrange("o (s n) -> o s n", n=P).bitcast(F32),
                                 r_row[4 * h:4 * h + 4, slot, :].bitcast(F32)).then_inc(r_loaded[slot], 16)

            load_q_max(0, 0, 0)
            for c in range(NCH):
                load_k_max(0, c)
            load_q(0, 0, 0)
            load_q_max(0, 1, 1)
            sp.wait_ge(k_two_set, 1)
            for c in range(NCH):
                load_k_and_v(0, c)
            sp.wait_ge(q_two_set, 1)
            load_r(0, 0)

            def queries_ahead(pair, t, slot, maxima=True):
                tile = NCH * pair + t
                sp.wait_ge(scores_ready, JT * tile + 1)
                if maxima:
                    load_q_max((tile + 2) // NCH, (tile + 2) % NCH, slot)
                load_q((tile + 1) // NCH, (tile + 1) % NCH, 1 - slot)

            def plain_tiles(pair):
                with sp.Fori(0, (NCH - 2) // 2, 1) as k:
                    for slot in range(2):
                        queries_ahead(pair, 2 * k + slot, slot)
                        load_r(NCH * pair + 2 * k + slot + 1, 1 - slot)

            with sp.Fori(0, HEADS // 2 - 1, 1) as pair:
                plain_tiles(pair)
                tile = NCH * pair + NCH - 2
                queries_ahead(pair, NCH - 2, 0)
                for c in range(NCH):
                    sp.wait_ge(max_ready, UNITS * (tile + 1) + 8 * (c + 1))
                    load_k_max(pair + 1, c)
                load_r(tile + 1, 1)
                tile = NCH * pair + NCH - 1
                queries_ahead(pair, NCH - 1, 1)
                for c in range(NCH):
                    if c == NCH - 1:
                        load_r(tile + 1, 0)
                    sp.wait_ge(scores_ready, JT * tile + 4 * (c + 1))
                    sp.wait_ge(probs_used, JT * tile + 4 * (c + 1))
                    load_k_and_v(pair + 1, c)
            plain_tiles(HEADS // 2 - 1)
            queries_ahead(HEADS // 2 - 1, NCH - 2, 0, maxima=False)
            load_r(TILES - 1, 1)

        @block.tensor
        def _(pe):
            pe.wait_ge(consts_loaded, 16)
            pe.wait_ge(ones_set, 1)
            pe.wait_ge(q_max_set, 1)

            def maximum_unit(tile, slot, u, start=False):
                c, h, s = u // 8, (u % 8) // 4, u % 4
                if u == 0:
                    pe.wait_ge(qm_loaded[slot], 16 * QM_DMAS * (tile // 2 + 1))
                if u % 8 == 0:
                    pe.wait_ge(km_loaded[c], 16 * KM_DMAS * (tile // NCH + 1))
                if not (start and u < 2):
                    pe.wait_ge(max_read, UNITS * tile + u - 1)
                nc.tensor.matmul(max_ps[:, u % 2, :], q_max[:, slot, h, s * P:(s + 1) * P],
                                 k_max[:, h, c * CH:(c + 1) * CH], start=True, stop=True).then_inc(max_ready, 1)

            def turn_maxima(tile, first=False):
                pe.wait_ge(r_ready, tile + 1)
                if not first:
                    pe.wait_ge(den_inverted, tile - 1)
                nc.tensor.matmul(misc_ps[0:2 * CH // P, 0:P], r_col[:, :], ident[:, :],
                                 start=True, stop=True).then_inc(r_turned, 1)

            def score(tile, slot, jt, h, start):
                if h == 0 and not (start and jt < 2):
                    pe.wait_ge(probs_ready, JT * tile + jt - 1)
                keys = slice(jt * P, (jt + 1) * P)
                nc.tensor.matmul(scores[:, jt % 2, h, :], k_one[:, h, keys], q_one[:, slot, h, :],
                                 start=True, stop=False)
                last = nc.tensor.matmul(scores[:, jt % 2, h, :], k_two[:, h, keys], q_two[:, slot, h, :],
                                        start=False, stop=True)
                if h == 1:
                    last.then_inc(scores_ready, 1)

            def times_v(tile, jt):
                pe.wait_ge(probs_ready, JT * tile + jt + 1)
                for h in range(2):
                    last = nc.tensor.matmul(out_ps[h * D:(h + 1) * D, :], v_sb[:, jt, h * D:(h + 1) * D],
                                            probs[:, jt % PSLOTS, h, :], start=(jt == 0), stop=(jt == JT - 1))
                last.then_inc(probs_used, 1)

            def denominators(tile):
                pe.wait_ge(den_summed, tile + 1)
                pe.wait_ge(r_copied, tile + 2 if tile is not TILES - 1 else TILES)
                for h in range(2):
                    last = nc.tensor.matmul(misc_ps[h * D:(h + 1) * D, :], ones[:, :], den_sum[:, h, :],
                                            start=True, stop=True)
                last.then_inc(den_ready, 1)

            def attend(tile, slot, start=False, maxima=True):
                pe.wait_ge(qab_loaded[slot], 16 * QAB_DMAS * (tile // 2 + 1))
                pe.wait_ge(r_loaded[slot], 32 * (tile // 2 + 1))
                for step in range(JT // 2):
                    if step % 2 == 0:
                        pe.wait_ge(kab_loaded[step // 2], 16 * KAB_DMAS * (tile // NCH + 1))
                    units = units_of(step) if maxima else ()
                    for i in range(4):
                        score(tile, slot, 2 * step + i // 2, i % 2, start)
                        for u in units[i:i + 1]:
                            maximum_unit(tile + 1, 1 - slot, u)
                    if step == 0 and not start:
                        for jt in (JT - 2, JT - 1):
                            times_v(tile - 1, jt)
                    if step == 1 and not start:
                        pe.wait_ge(out_copied, tile)
                    if step >= 1:
                        for jt in (2 * step - 2, 2 * step - 1):
                            times_v(tile, jt)
                    for u in units[4:]:
                        maximum_unit(tile + 1, 1 - slot, u)
                    if step == 3 and not start:
                        denominators(tile - 1)
                    if step == JT // 2 - 2 and maxima:
                        turn_maxima(tile + 1)

            for u in range(UNITS):
                maximum_unit(0, 0, u, start=True)
            turn_maxima(0, first=True)
            attend(0, 0, start=True)
            attend(1, 1)
            attend(2, 0)
            with pe.Fori(0, (TILES - 4) // 2, 1) as k:
                attend(2 * k + 3, 1)
                attend(2 * k + 4, 0)
            attend(TILES - 1, 1, maxima=False)
            for jt in (JT - 2, JT - 1):
                times_v(TILES - 1, jt)
            denominators(TILES - 1)

        @block.scalar
        def _(act):
            def exponentials(tile, jt, start):
                act.wait_ge(scores_ready, JT * tile + jt + 1)
                if not (start and jt < PSLOTS):
                    act.wait_ge(probs_used, JT * tile + jt - PSLOTS + 1)
                    before = tile if jt >= PSLOTS else tile - 1
                    j = (jt - PSLOTS) % JT
                    if j in POOL_JTS:
                        act.wait_ge(pool_added, POOL_OPS * before + pool_ops_through(j))
                    else:
                        act.wait_ge(dve_added, DVE_OPS * before + dve_ops_through(j))
                nc.scalar.activation(probs[:, jt % PSLOTS, :, :], scores[:, jt % 2, :, :], ACT.Exp,
                                     scale=0.25).then_inc(probs_ready, 1)

            def copy_out(tile, first=False):
                act.wait_ge(probs_used, JT * (tile + 1))
                if not first:
                    act.wait_ge(normalised, tile)
                nc.scalar.copy(out_raw[:, :], out_ps[:, :]).then_inc(out_copied, 1)

            def store(tile, slot):
                act.wait_ge(normalised, tile + 1)
                act.dma_start(o_s[tile, :, :], out_norm[:, slot, :]).then_inc(out_stored[slot], 16)

            def attend(tile, slot, start=False, second=False):
                for jt in range(JT):
                    exponentials(tile, jt, start)
                    if jt == 1 and not start:
                        copy_out(tile - 1)
                    if jt == JT - 1 and not start:
                        store(tile - 1, 1 - slot)

            attend(0, 0, start=True)
            attend(1, 1)
            attend(2, 0)
            with act.Fori(0, (TILES - 4) // 2, 1) as k:
                attend(2 * k + 3, 1)
                attend(2 * k + 4, 0)
            attend(TILES - 1, 1)
            copy_out(TILES - 1)
            store(TILES - 1, 1)
            for s in range(2):
                act.wait_ge(out_stored[s], 16 * TILES // 2)

        @block.vector
        def _(dve):
            nc.vector.memset(q_max[D:D + 2, :, :, :].bitcast(F32), 1.0).then_inc(q_max_set, 1)
            nc.vector.memset(ones[:, :], 1.0).then_inc(ones_set, 1)

            def maximum_unit(tile, u, first=False):
                c, h, s = u // 8, (u % 8) // 4, u % 4
                if u == 0 and not first:
                    dve.wait_ge(r_ready, tile)
                dve.wait_ge(max_ready, UNITS * tile + u + 1)
                nc.vector.tensor_reduce(row_max[:, 4 * h + s, c:c + 1], max_ps[:, u % 2, :], AX.X,
                                        ALU.max).then_inc(max_read, 1)

            def row_maxima(tile, first=False):
                dve.wait_ge(max_read, UNITS * (tile + 1))
                if not first:
                    dve.wait_ge(r_turned, tile)
                nc.vector.tensor_reduce(r_col[:, :], row_max[:, :, :], AX.X, ALU.max).then_inc(r_ready, 1)

            def copy_maxima(tile, half):
                slot = half[1]
                dve.wait_ge(r_turned, tile + 1)
                dve.wait_ge(r_loaded[slot], 32 * half[0])
                nc.vector.tensor_scalar(r_row[:, slot, :], misc_ps[0:2 * CH // P, 0:P], -1.0, None,
                                        ALU.mult).then_inc(r_copied, 1)

            def add(tile, jt):
                if jt not in DVE_JTS[1:]:
                    return
                k = DVE_JTS.index(jt)
                dve.wait_ge(probs_ready, JT * tile + jt + 1)
                dve.wait_ge(dve_added, DVE_OPS * tile + k - 1)
                before = probs[:, DVE_JTS[0], :, :] if k == 1 else den_dve[:, :, :]
                nc.vector.tensor_tensor(den_dve[:, :, :], before, probs[:, jt % PSLOTS, :, :],
                                        ALU.add).then_inc(dve_added, 1)

            def sum_denominators(tile):
                dve.wait_ge(dve_added, DVE_OPS * (tile + 1))
                dve.wait_ge(pool_added, POOL_OPS * (tile + 1))
                dve.wait_ge(den_ready, tile)
                nc.vector.tensor_tensor(den_sum[:, :, :], den_dve[:, :, :], den_pool[:, :, :],
                                        ALU.add).then_inc(den_summed, 1)
                dve.wait_ge(den_summed, tile + 1)

            def normalise(tile, half):
                slot = half[1]
                dve.wait_ge(den_ready, tile + 1)
                dve.wait_ge(normalised, tile)
                nc.vector.reciprocal(den_inv[:, :], misc_ps[:, :]).then_inc(den_inverted, 1)
                dve.wait_ge(den_inverted, tile + 1)
                dve.wait_ge(out_copied, tile + 1)
                dve.wait_ge(out_stored[slot], 16 * half[0])
                nc.vector.tensor_tensor(out_norm[:, slot, :], out_raw[:, :], den_inv[:, :],
                                        ALU.mult).then_inc(normalised, 1)

            def attend(k, slot, start=False, maxima=True):
                tile = 2 * k + slot
                before = (k, 0) if slot else (k - 1, 1)
                after = (k + 1, 0) if slot else (k, 1)
                for step in range(JT // 2):
                    units = units_of(step) if maxima else ()
                    for u in units[:4]:
                        maximum_unit(tile + 1, u)
                    if step == 0 and not start:
                        for jt in (JT - 2, JT - 1):
                            add(tile - 1, jt)
                    if step == 1 and not start:
                        sum_denominators(tile - 1)
                    if step >= 1:
                        for jt in (2 * step - 2, 2 * step - 1):
                            add(tile, jt)
                    for u in units[4:]:
                        maximum_unit(tile + 1, u)
                    if UNITS - 1 in units:
                        row_maxima(tile + 1)
                    if step == JT // 2 - 3 and not start:
                        normalise(tile - 1, before)
                    if step == JT // 2 - 1 and maxima:
                        copy_maxima(tile + 1, after)

            for u in range(UNITS):
                maximum_unit(0, u, first=True)
            row_maxima(0, first=True)
            copy_maxima(0, (0, 0))
            attend(0, 0, start=True)
            attend(0, 1)
            attend(1, 0)
            with dve.Fori(0, (TILES - 4) // 2, 1) as k:
                attend(k + 1, 1)
                attend(k + 2, 0)
            attend(TILES // 2 - 1, 1, maxima=False)
            for jt in (JT - 2, JT - 1):
                add(TILES - 1, jt)
            sum_denominators(TILES - 1)
            normalise(TILES - 1, (TILES // 2 - 1, 1))

        @block.gpsimd
        def _(pool):
            nc.gpsimd.memset(q_two[D:D + 3, :, :, :].bitcast(F32), 1.0).then_inc(q_two_set, 1)
            nc.gpsimd.memset(k_two[D:D + 3, :, :].bitcast(F32), 1.0).then_inc(k_two_set, 1)

            def add_up(tile):
                for k, jt in enumerate(POOL_JTS[1:], 1):
                    pool.wait_ge(probs_ready, JT * tile + jt + 1)
                    pool.wait_ge(pool_added, POOL_OPS * tile + k - 1)
                    if k == 1:
                        pool.wait_ge(den_summed, tile)
                    before = probs[:, POOL_JTS[0], :, :] if k == 1 else den_pool[:, :, :]
                    nc.gpsimd.tensor_tensor(den_pool[:, :, :], before, probs[:, jt % PSLOTS, :, :],
                                            ALU.add).then_inc(pool_added, 1)

            add_up(0)
            with pool.Fori(0, TILES - 1, 1) as k:
                add_up(k + 1)


def output_and_convolution(nc, x, wo_t, gmat_d, taps_d, o_s, z):
    with ExitStack() as ctx:
        def sb(name, shape, dt=F32):
            return ctx.enter_context(nc.sbuf_tensor(name, shape, dt))

        def sem(name):
            return ctx.enter_context(nc.semaphore(name))

        y_sb = sb("p3_y", [P, CT, N])
        w_raw = sb("p3_w_raw", [P, CT, C])
        w_hi = sb("p3_w_hi", [P, CT, C], F32R)
        w_lo = sb("p3_w_lo", [P, CT, C], F32R)
        o_raw = sb("p3_o_raw", [P, 2, CT, CH])
        o_hi = sb("p3_o_hi", [P, 2, CT, CH], F32R)
        o_lo = sb("p3_o_lo", [P, 2, CT, CH], F32R)
        x_res = sb("p3_x_res", [P, 2, CT, CH])
        gmat = sb("p3_gmat", [P, P])
        taps = sb("p3_taps", [P, 3 * P])
        stats = sb("p3_stats", [P, CT, NCH, 6])
        mv = sb("p3_mv", [P, CT, 2])
        ex = sb("p3_ex", [P, CT, 2])
        root = sb("p3_root", [P, CT, 2])
        mean = sb("p3_mean", [P, CT])
        rstd = sb("p3_rstd", [P, CT])
        acc = ctx.enter_context(nc.psum_tensor("p3_acc", [P, CT, CH], F32))
        gn_ps = ctx.enter_context(nc.psum_tensor("p3_gn", [P, CT, 2], F32))
        yn, z_st = o_raw, x_res

        consts_loaded = sem("p3_consts_loaded")
        w_loaded = sem("p3_w_loaded")
        w_hi_done = sem("p3_w_hi_done")
        w_lo_done = sem("p3_w_lo_done")
        o_loaded = [sem(f"p3_o_loaded{s}") for s in range(2)]
        x_loaded = [sem(f"p3_x_loaded{s}") for s in range(2)]
        o_hi_done = sem("p3_o_hi_done")
        o_lo_done = sem("p3_o_lo_done")
        wo_ready = sem("p3_wo_ready")
        y_done = sem("p3_y_done")
        stats_done = sem("p3_stats_done")
        gn_ready = sem("p3_gn_ready")
        yn_done = sem("p3_yn_done")
        conv_ready = sem("p3_conv_ready")
        z_done = sem("p3_z_done")
        z_stored = [sem(f"p3_z_stored{s}") for s in range(2)]
        gn_vector, gn_tensor, gn_scalar = group_statistics(
            nc, None, lambda n: sem("p3_" + n), None, stats, mv, ex, gn_ps, gmat, root, mean, rstd, gn_ready)
        block = ctx.enter_context(nc.Block())

        @block.sync
        def _(sp):
            def load(n, slot):
                sp.dma_start(o_raw[:, slot, :, :],
                             o_s.rearrange("(q t) p n -> t p q n", t=NCH)[n, :, :, :]).then_inc(o_loaded[slot], 16)
                sp.dma_start(x_res[:, slot, :, :],
                             x[:, bass.ts(n, CH)].rearrange("(m p) n -> p m n", p=P)).then_inc(x_loaded[slot], 16)

            for n in range(2):
                load(n, n)
            sp.dma_start(gmat[:, :], gmat_d).then_inc(consts_loaded, 16)
            sp.dma_start(taps[:, :], bass.AP(tensor=taps_d.tensor, offset=P - 1,
                                             ap=[[C - 1, P], [1, 3 * P]])).then_inc(consts_loaded, 16)
            with sp.Fori(0, (NCH - 2) // 2, 1) as k:
                for slot in range(2):
                    sp.wait_ge(y_done, CT * (2 * k + slot + 1))
                    sp.wait_ge(o_lo_done, 2 * k + slot + 1)
                    load(2 * k + slot + 2, slot)
            with sp.Fori(0, NCH // 2, 1) as k:
                for slot in range(2):
                    sp.wait_ge(z_done, CT * (2 * k + slot + 1))
                    sp.dma_start(z[:, bass.ts(2 * k + slot, CH)].rearrange("(m p) n -> p m n", p=P),
                                 z_st[:, slot, :, :]).then_inc(z_stored[slot], 16)
            for s in range(2):
                sp.wait_ge(z_stored[s], 16 * NCH // 2)

        @block.scalar
        def _(act):
            act.dma_start(w_raw[:, :, :], wo_t.rearrange("(m p) o -> p m o", p=P)).then_inc(w_loaded, 16)
            act.wait_ge(w_loaded, 16)
            nc.scalar.copy(w_hi[:, :, :], w_raw[:, :, :]).then_inc(w_hi_done, 1)

            def split(k, slot):
                act.wait_ge(o_loaded[slot], 16 * (k + 1))
                act.wait_ge(wo_ready, 8 * k)
                nc.scalar.copy(o_hi[:, slot, :, :], o_raw[:, slot, :, :]).then_inc(o_hi_done, 1)

            split(0, 0)
            split(0, 1)
            with act.Fori(0, NCH // 2 - 1, 1) as k:
                split(k + 1, 0)
                split(k + 1, 1)
            gn_scalar(act)

        @block.vector
        def _(dve):
            dve.wait_ge(w_hi_done, 1)
            nc.vector.tensor_tensor(w_lo[:, :, :], w_raw[:, :, :], w_hi[:, :, :].bitcast(F32),
                                    ALU.subtract).then_inc(w_lo_done, 1)

            def split(n, slot):
                dve.wait_ge(o_hi_done, n + 1)
                nc.vector.tensor_tensor(o_lo[:, slot, :, :], o_raw[:, slot, :, :],
                                        o_hi[:, slot, :, :].bitcast(F32), ALU.subtract).then_inc(o_lo_done, 1)

            def residual(n, k, slot):
                dve.wait_ge(x_loaded[slot], 16 * (k + 1))
                for m in range(CT):
                    dve.wait_ge(wo_ready, CT * n + m + 1)
                    nc.vector.scalar_tensor_tensor(
                        out=y_sb[:, m, bass.ts(n, CH)], in0=acc[:, m, :], scalar=GAIN,
                        in1=x_res[:, slot, m, :], op0=ALU.mult, op1=ALU.add).then_inc(y_done, 1)
                dve.wait_ge(y_done, CT * (n + 1))
                for m in range(CT):
                    nc.vector.bn_stats(stats[:, m, n, :], y_sb[:, m, bass.ts(n, CH)]).then_inc(stats_done, 1)

            split(0, 0)
            with dve.Fori(0, NCH // 2 - 1, 1) as k:
                split(2 * k + 1, 1)
                residual(2 * k, k, 0)
                split(2 * k + 2, 0)
                residual(2 * k + 1, k, 1)
            split(NCH - 1, 1)
            residual(NCH - 2, NCH // 2 - 1, 0)
            residual(NCH - 1, NCH // 2 - 1, 1)
            dve.wait_ge(stats_done, CT * NCH)
            gn_vector(dve)

            def normalise(n, slot, start=False):
                if not start:
                    dve.wait_ge(conv_ready, CT * (n - 1))
                for m in range(CT):
                    nc.vector.tensor_scalar(yn[:, slot, m, :], y_sb[:, m, bass.ts(n, CH)], mean[:, m:m + 1],
                                            rstd[:, m:m + 1], ALU.subtract, ALU.mult).then_inc(yn_done, 1)

            def finish(n, k, slot):
                dve.wait_ge(z_stored[slot], 16 * k)
                for m in range(CT):
                    dve.wait_ge(conv_ready, CT * n + m + 1)
                    nc.vector.tensor_tensor(z_st[:, slot, m, :], acc[:, m, :], y_sb[:, m, bass.ts(n, CH)],
                                            ALU.add).then_inc(z_done, 1)

            normalise(0, 0, start=True)
            normalise(1, 1, start=True)
            finish(0, 0, 0)
            normalise(2, 0)
            finish(1, 0, 1)
            normalise(3, 1)
            with dve.Fori(0, NCH // 2 - 2, 1) as k:
                finish(2 * k + 2, k + 1, 0)
                normalise(2 * k + 4, 0)
                finish(2 * k + 3, k + 1, 1)
                normalise(2 * k + 5, 1)
            finish(NCH - 2, NCH // 2 - 1, 0)
            finish(NCH - 1, NCH // 2 - 1, 1)

        @block.tensor
        def _(pe):
            def project(k, slot):
                pe.wait_ge(o_lo_done, 2 * k + slot + 1)
                for m in range(CT):
                    pe.wait_ge(y_done, 8 * k + (m + 1 if slot else 0))
                    cols = slice(m * P, (m + 1) * P)
                    for i in range(3 * CT):
                        c, term = divmod(i, 3)
                        last = nc.tensor.matmul(acc[:, m, :],
                                                (w_lo if term == 2 else w_hi)[:, c, cols],
                                                (o_lo if term == 1 else o_hi)[:, slot, c, :],
                                                start=(i == 0), stop=(i == 3 * CT - 1))
                    last.then_inc(wo_ready, 1)

            def convolve(k, slot):
                pe.wait_ge(yn_done, CT * (2 * k + slot + 1))
                for m in range(CT):
                    pe.wait_ge(z_done, 8 * k + (m + 1 if slot else 0))
                    nc.tensor.matmul(acc[:, m, :], taps[:, 2 * P:3 * P],
                                     yn[:, slot, (m - 1) % CT, :], start=True, stop=False)
                    nc.tensor.matmul(acc[:, m, :], taps[:, P:2 * P], yn[:, slot, m, :],
                                     start=False, stop=False)
                    nc.tensor.matmul(acc[:, m, :], taps[:, 0:P], yn[:, slot, (m + 1) % CT, :],
                                     start=False, stop=True).then_inc(conv_ready, 1)

            pe.wait_ge(w_lo_done, 1)
            project(0, 0)
            project(0, 1)
            with pe.Fori(0, NCH // 2 - 1, 1) as k:
                project(k + 1, 0)
                project(k + 1, 1)
            pe.wait_ge(consts_loaded, 32)
            gn_tensor(pe)
            pe.wait_ge(y_done, CT * NCH)
            convolve(0, 0)
            convolve(0, 1)
            with pe.Fori(0, NCH // 2 - 1, 1) as k:
                convolve(k + 1, 0)
                convolve(k + 1, 1)


def build(nc, x, wq_t, wk_t, wv_t, wo_t, taps, gmat, sel, ident, z):
    q_s = nc.dram_tensor("q_scratch", [HEADS, 2, D, N], F32, kind="Internal").ap()
    k_s = nc.dram_tensor("k_scratch", [HEADS, 2, D, N], F32, kind="Internal").ap()
    v_s = nc.dram_tensor("v_scratch", [HEADS // 2, P, JT, P], F32, kind="Internal").ap()
    aa_s = nc.dram_tensor("aa_scratch", [HEADS, 2, N], F32, kind="Internal").ap()
    o_s = nc.dram_tensor("o_scratch", [TILES, P, CH], F32, kind="Internal").ap()
    projections(nc, x, wq_t, wk_t, wv_t, gmat, sel, q_s, k_s, v_s, aa_s)
    attention(nc, ident, q_s, k_s, v_s, aa_s, o_s)
    output_and_convolution(nc, x, wo_t, gmat, taps, o_s, z)


def kernel(x, L0_conv_wq, L0_conv_wk, L0_conv_wv, L0_conv_wo, L1_conv_inhibition_filter):
    import numpy as np
    import concourse.bacc as bacc
    from concourse.bass_utils import run_bass_kernel_spmd

    left = (C - SCOPE) // 2
    padded = np.pad(np.asarray(L1_conv_inhibition_filter)[0, 0], (left, C - SCOPE - left))
    channel = np.arange(P)
    arrays = {
        "x_in": np.ascontiguousarray(np.asarray(x).reshape(C, N)),
        "wq_t": np.ascontiguousarray(np.asarray(L0_conv_wq).T),
        "wk_t": np.ascontiguousarray(np.asarray(L0_conv_wk).T),
        "wv_t": np.ascontiguousarray(np.asarray(L0_conv_wv).T),
        "wo_t": np.ascontiguousarray(np.asarray(L0_conv_wo).T),
        "taps": np.ascontiguousarray(np.broadcast_to(padded, (P, C))),
        "gmat": (channel[:, None] // 16 == channel[None, :] // 16).astype(np.float32) / 16,
        "sel": np.where(channel[:, None] // D == np.arange(2)[None, :], -0.5, 0.0).astype(np.float32),
        "ident": np.eye(P, dtype=np.float32),
    }
    nc = bacc.Bacc("TRN2", target_bir_lowering=False, num_devices=1)
    args = [nc.dram_tensor(k, a.shape, F32, kind="ExternalInput").ap() for k, a in arrays.items()]
    z = nc.dram_tensor("z_out", (C, N), F32, kind="ExternalOutput").ap()
    build(nc, *args, z)
    r = run_bass_kernel_spmd(nc, [arrays], core_ids=[0])
    return r.results[0]["z_out"].reshape(1, C, 64, 64)
```

```python
from contextlib import ExitStack

import concourse.bass as bass
from concourse import mybir

F32 = mybir.dt.float32
F32R = mybir.dt.float32r
ALU = mybir.AluOpType
ACT = mybir.ActivationFunctionType
AX = mybir.AxisListType

C = 512
N = 4096
HEADS = 8
D = C // HEADS
P = 128
CT = C // P
CH = 512
NCH = N // CH
GAIN = float(C) ** -0.5
SCOPE = 63
GN_EPS = 1e-5

TILES = (HEADS // 2) * NCH
JT = N // P
UNITS = 2 * (CH // P) * NCH
UNITS_PER_STEP = 5
PSLOTS = 8
POOL_SLOTS = (1, 2, 3, 5, 6, 7)
DVE_JTS = [j for j in range(JT) if j % PSLOTS not in POOL_SLOTS]
POOL_JTS = [j for j in range(JT) if j % PSLOTS in POOL_SLOTS]
DVE_OPS = len(DVE_JTS) - 1
POOL_OPS = len(POOL_JTS) - 1
KM_DMAS, KAB_DMAS, QM_DMAS, QAB_DMAS = 4, 7, 2, 6


def wait(engine, semaphore, count):
    if not isinstance(count, int) or count > 0:
        engine.wait_ge(semaphore, count)


def group_statistics(nc, sem, stats, mv, ex, psum, gmat, root, mean, rstd, ready):
    step = sem("gn_step")
    sums = sem("gn_sums")
    rooted = sem("gn_root")

    def vector(dve):
        for m in range(CT):
            nc.vector.bn_aggr(mv[:, m, :], stats[:, m, :, :]).then_inc(step, 1)
        dve.wait_ge(step, CT)
        nc.vector.tensor_tensor(ex[:, :, 0], mv[:, :, 0], mv[:, :, 0], ALU.mult).then_inc(step, 1)
        dve.wait_ge(step, CT + 1)
        nc.vector.tensor_tensor(mv[:, :, 1], mv[:, :, 1], ex[:, :, 0], ALU.add).then_inc(step, 1)
        dve.wait_ge(sums, 1)
        nc.vector.tensor_copy(mean[:, :], psum[:, :, 0]).then_inc(step, 1)
        dve.wait_ge(step, CT + 3)
        nc.vector.tensor_tensor(ex[:, :, 0], mean[:, :], mean[:, :], ALU.mult).then_inc(step, 1)
        dve.wait_ge(step, CT + 4)
        nc.vector.tensor_tensor(ex[:, :, 1], psum[:, :, 1], ex[:, :, 0], ALU.subtract).then_inc(step, 1)
        dve.wait_ge(step, CT + 5)
        nc.vector.tensor_scalar(root[:, :, 0], ex[:, :, 1], GN_EPS, None, ALU.add).then_inc(step, 1)
        dve.wait_ge(rooted, 1)
        nc.vector.reciprocal(ex[:, :, 0], root[:, :, 1]).then_inc(step, 1)
        dve.wait_ge(step, CT + 7)
        nc.vector.tensor_tensor(ex[:, :, 1], root[:, :, 0], ex[:, :, 0], ALU.mult).then_inc(step, 1)
        dve.wait_ge(step, CT + 8)
        nc.vector.tensor_tensor(ex[:, :, 0], ex[:, :, 1], root[:, :, 1], ALU.add).then_inc(step, 1)
        dve.wait_ge(step, CT + 9)
        nc.vector.tensor_scalar(ex[:, :, 1], ex[:, :, 0], 0.5, None, ALU.mult).then_inc(step, 1)
        dve.wait_ge(step, CT + 10)
        nc.vector.reciprocal(rstd[:, :], ex[:, :, 1]).then_inc(ready, 1)
        dve.wait_ge(ready, 1)

    def tensor(pe):
        pe.wait_ge(step, CT + 2)
        nc.tensor.matmul(psum[:, :, :].rearrange("p m s -> p (m s)"), gmat[:, :],
                         mv[:, :, :].rearrange("p m s -> p (m s)"), start=True, stop=True).then_inc(sums, 1)

    def scalar(act):
        act.wait_ge(step, CT + 6)
        nc.scalar.activation(root[:, :, 1], root[:, :, 0], ACT.Sqrt).then_inc(rooted, 1)

    return vector, tensor, scalar


def projections(nc, x, wq_t, wk_t, wv_t, gmat_d, sel_d, q_s, k_s, v_s, aa_s):
    with ExitStack() as ctx:
        def sb(name, shape, dt=F32):
            return ctx.enter_context(nc.sbuf_tensor(name, shape, dt))

        def sem(name):
            return ctx.enter_context(nc.semaphore(name))

        x_sb = sb("p1_x", [P, CT, N])
        w_hi = sb("p1_w_hi", [P, 3, CT, C], F32R)
        w_lo = sb("p1_w_lo", [P, 3, CT, C], F32R)
        w_raw = sb("p1_w_raw", [P, 2, CT, C])
        xn = sb("p1_xn", [P, CT, CH])
        xn_hi = sb("p1_xn_hi", [P, 2, CT, CH], F32R)
        xn_lo = sb("p1_xn_lo", [P, 2, CT, CH], F32R)
        qk_st = sb("p1_qk_st", [P, 2, 2, CH], F32R)
        v_st = sb("p1_v_st", [P, 2, CH])
        sq = sb("p1_sq", [P, 2, CH])
        sq_hi = sb("p1_sq_hi", [P, 2, CH], F32R)
        sq_lo = sb("p1_sq_lo", [P, 2, CH], F32R)
        aa_st = sb("p1_aa_st", [HEADS, 2, 2, CH], F32R)
        gmat = sb("p1_gmat", [P, P])
        sel_raw = sb("p1_sel_raw", [P, CT, P])
        sel = sb("p1_sel", [P, CT, P], F32R)
        stats = sb("p1_stats", [P, CT, NCH, 6])
        mv = sb("p1_mv", [P, CT, 2])
        ex = sb("p1_ex", [P, CT, 2])
        root = sb("p1_root", [P, CT, 2])
        mean = sb("p1_mean", [P, CT])
        rstd = sb("p1_rstd", [P, CT])
        acc = ctx.enter_context(nc.psum_tensor("p1_acc", [P, 4, CH], F32))
        aa_ps = ctx.enter_context(nc.psum_tensor("p1_aa", [P, CH], F32))
        gn_ps = ctx.enter_context(nc.psum_tensor("p1_gn", [P, CT, 2], F32))

        x_loaded = [sem(f"p1_x_loaded{m}") for m in range(CT)]
        consts_loaded = sem("p1_consts_loaded")
        w_loaded = [sem(f"p1_w_loaded{w}") for w in range(3)]
        sel_done = sem("p1_sel_done")
        w_hi_done = sem("p1_w_hi_done")
        w_lo_done = sem("p1_w_lo_done")
        stats_done = sem("p1_stats_done")
        gn_ready = sem("p1_gn_ready")
        xn_done = sem("p1_xn_done")
        xn_hi_done = sem("p1_xn_hi_done")
        xn_lo_done = sem("p1_xn_lo_done")
        qk_ready = sem("p1_qk_ready")
        v_ready = sem("p1_v_ready")
        sq_used = sem("p1_sq_used")
        qk_hi_done = sem("p1_qk_hi_done")
        qk_lo_done = sem("p1_qk_lo_done")
        sq_done = sem("p1_sq_done")
        sq_lo_done = sem("p1_sq_lo_done")
        v_done = sem("p1_v_done")
        aa_hi_done = sem("p1_aa_hi_done")
        aa_lo_done = sem("p1_aa_lo_done")
        qk_stored = [sem(f"p1_qk_stored{s}") for s in range(2)]
        v_stored = [sem(f"p1_v_stored{s}") for s in range(2)]
        aa_stored = [sem(f"p1_aa_stored{s}") for s in range(2)]
        gn_vector, gn_tensor, gn_scalar = group_statistics(
            nc, lambda n: sem("p1_" + n), stats, mv, ex, gn_ps, gmat, root, mean, rstd, gn_ready)
        block = ctx.enter_context(nc.Block())
        weights = (wq_t, wk_t, wv_t)

        def wait_bank(pe, n, p):
            m, kind = divmod((p - 4) % 12, 3)
            before = n if p >= 4 else n - 1
            if kind == 2:
                wait(pe, v_done, 4 * before + m + 1)
            else:
                wait(pe, qk_lo_done, 8 * before + 2 * m + kind + 1)

        @block.sync
        def _(sp):
            sp.dma_start(gmat[:, :], gmat_d).then_inc(consts_loaded, 16)
            sp.dma_start(sel_raw[:, :, :], sel_d).then_inc(consts_loaded, 16)
            for m in range(CT):
                for half in range(2):
                    cols = slice(half * N // 2, (half + 1) * N // 2)
                    sp.dma_start(x_sb[:, m, cols], x[m * P:(m + 1) * P, cols]).then_inc(x_loaded[m], 16)
                if m >= 1:
                    wait(sp, w_lo_done, m - 2)
                    sp.dma_start(w_raw[:, (m - 1) % 2, :, :],
                                 weights[m - 1].rearrange("(c p) o -> p c o", p=P)).then_inc(w_loaded[m - 1], 16)
            def store(k, slot):
                n = 2 * k + slot
                for m in range(CT):
                    for kind, dst in enumerate((q_s, k_s)):
                        sp.wait_ge(qk_lo_done, 8 * n + 2 * m + kind + 1)
                        for h in range(2):
                            sp.dma_start(dst[2 * m + h, :, :, bass.ts(n, CH)].rearrange("s c n -> c s n"),
                                         qk_st[h * D:(h + 1) * D, kind, :, :].bitcast(F32)
                                         ).then_inc(qk_stored[kind], 16)
                    sp.wait_ge(v_done, 4 * n + m + 1)
                    sp.dma_start(v_s[:, :, 4 * n + m, :].rearrange("q p d -> p q d"),
                                 v_st[:, m % 2, :].rearrange("p (q d) -> p q d", q=CT)
                                 ).then_inc(v_stored[m % 2], 16)
                sp.wait_ge(aa_lo_done, n + 1)
                sp.dma_start(aa_s[:, :, bass.ts(n, CH)], aa_st[:, slot, :, :].bitcast(F32)).then_inc(aa_stored[slot], 16)

            with sp.Fori(0, NCH // 2, 1) as k:
                store(k, 0)
                store(k, 1)
            for s in range(2):
                sp.wait_ge(qk_stored[s], 32 * CT * NCH)
                sp.wait_ge(v_stored[s], 16 * CT * NCH // 2)
                sp.wait_ge(aa_stored[s], 16 * NCH // 2)

        @block.scalar
        def _(act):
            act.wait_ge(consts_loaded, 32)
            nc.scalar.copy(sel[:, :, :], sel_raw[:, :, :]).then_inc(sel_done, 1)

            def weight_hi(w):
                act.wait_ge(w_loaded[w], 16)
                nc.scalar.copy(w_hi[:, w, :, :], w_raw[:, w % 2, :, :]).then_inc(w_hi_done, 1)

            def normalised_hi(n, slot):
                act.wait_ge(xn_done, CT * (n + 1))
                wait(act, qk_ready, 8 * (n - 1))
                wait(act, v_ready, 4 * (n - 1))
                nc.scalar.copy(xn_hi[:, slot, :, :], xn[:, :, :]).then_inc(xn_hi_done, 1)

            def evacuate(k, slot, prepare=True):
                n = 2 * k + slot
                for m in range(CT):
                    for kind in range(2):
                        p = 3 * m + kind
                        act.wait_ge(qk_ready, 8 * n + 2 * m + kind + 1)
                        wait(act, qk_stored[kind], 32 * (4 * n + m))
                        nc.scalar.mul(qk_st[:, kind, 0, :], acc[:, p % 4, :], GAIN).then_inc(qk_hi_done, 1)
                        if kind == 0:
                            wait(act, sq_lo_done, 4 * n + m - 1)
                            wait(act, sq_used, 4 * n + m - 1)
                            for part in (sq, sq_hi):
                                nc.scalar.activation(part[:, m % 2, :], acc[:, p % 4, :], ACT.Square,
                                                     scale=GAIN).then_inc(sq_done, 1)
                    act.wait_ge(v_ready, 4 * n + m + 1)
                    wait(act, v_stored[m % 2], 16 * (2 * n + m // 2))
                    nc.scalar.mul(v_st[:, m % 2, :], acc[:, (3 * m + 2) % 4, :], GAIN).then_inc(v_done, 1)
                    if m == 1 and prepare:
                        normalised_hi(n + 1, 1 - slot)
                act.wait_ge(sq_used, 4 * (n + 1))
                wait(act, aa_stored[slot], 16 * k)
                nc.scalar.copy(aa_st[:, slot, 0, :], aa_ps[0:HEADS, :]).then_inc(aa_hi_done, 1)

            weight_hi(0)
            weight_hi(1)
            gn_scalar(act)
            normalised_hi(0, 0)
            weight_hi(2)
            normalised_hi(1, 1)
            evacuate(0, 0, prepare=False)
            evacuate(0, 1)
            evacuate(1, 0)
            with act.Fori(0, NCH // 2 - 2, 1) as k:
                evacuate(k + 1, 1)
                evacuate(k + 2, 0)
            evacuate(NCH // 2 - 1, 1, prepare=False)

        @block.vector
        def _(dve):
            def weight_lo(w):
                dve.wait_ge(w_hi_done, w + 1)
                nc.vector.tensor_tensor(w_lo[:, w, :, :], w_raw[:, w % 2, :, :], w_hi[:, w, :, :].bitcast(F32),
                                        ALU.subtract).then_inc(w_lo_done, 1)

            for m in range(CT):
                dve.wait_ge(x_loaded[m], 32)
                for k in range(NCH):
                    nc.vector.bn_stats(stats[:, m, k, :], x_sb[:, m, k * CH:(k + 1) * CH]).then_inc(stats_done, 1)
                if m >= 2:
                    weight_lo(m - 2)
            dve.wait_ge(stats_done, CT * NCH)
            gn_vector(dve)

            def normalise(n):
                wait(dve, xn_lo_done, n)
                for m in range(CT):
                    nc.vector.tensor_scalar(xn[:, m, :], x_sb[:, m, bass.ts(n, CH)], mean[:, m:m + 1],
                                            rstd[:, m:m + 1], ALU.subtract, ALU.mult).then_inc(xn_done, 1)

            def normalised_lo(n, slot):
                dve.wait_ge(xn_hi_done, n + 1)
                dve.wait_ge(xn_done, CT * (n + 1))
                nc.vector.tensor_tensor(xn_lo[:, slot, :, :], xn[:, :, :], xn_hi[:, slot, :, :].bitcast(F32),
                                        ALU.subtract).then_inc(xn_lo_done, 1)

            def evacuate(k, slot, prepare=True):
                n = 2 * k + slot
                for m in range(CT):
                    if m == 0 and prepare:
                        normalise(n + 1)
                    for kind in range(2):
                        dve.wait_ge(qk_hi_done, 8 * n + 2 * m + kind + 1)
                        if kind == 0:
                            dve.wait_ge(sq_done, 2 * (4 * n + m + 1))
                        nc.vector.scalar_tensor_tensor(
                            out=qk_st[:, kind, 1, :], in0=acc[:, (3 * m + kind) % 4, :], scalar=GAIN,
                            in1=qk_st[:, kind, 0, :].bitcast(F32), op0=ALU.mult,
                            op1=ALU.subtract).then_inc(qk_lo_done, 1)
                    if m == 1 and prepare:
                        normalised_lo(n + 1, 1 - slot)
                dve.wait_ge(aa_hi_done, n + 1)
                nc.vector.tensor_tensor(aa_st[:, slot, 1, :], aa_ps[0:HEADS, :],
                                        aa_st[:, slot, 0, :].bitcast(F32), ALU.subtract).then_inc(aa_lo_done, 1)

            normalise(0)
            normalised_lo(0, 0)
            weight_lo(2)
            normalise(1)
            normalised_lo(1, 1)
            evacuate(0, 0, prepare=False)
            with dve.Fori(0, NCH // 2 - 1, 1) as k:
                evacuate(k, 1)
                evacuate(k + 1, 0)
            evacuate(NCH // 2 - 1, 1, prepare=False)

        @block.gpsimd
        def _(pool):
            def split_squares(n):
                for m in range(CT):
                    pool.wait_ge(sq_done, 2 * (4 * n + m + 1))
                    wait(pool, sq_used, 4 * n + m - 1)
                    nc.gpsimd.tensor_tensor(sq_lo[:, m % 2, :], sq[:, m % 2, :],
                                            sq_hi[:, m % 2, :].bitcast(F32), ALU.subtract).then_inc(sq_lo_done, 1)

            split_squares(0)
            with pool.Fori(0, NCH - 1, 1) as k:
                split_squares(k + 1)

        @block.tensor
        def _(pe):
            pe.wait_ge(consts_loaded, 32)
            gn_tensor(pe)

            def group(n, slot, p):
                m, kind = divmod(p, 3)
                if isinstance(n, int) and n == 0:
                    pe.wait_ge(w_lo_done, kind + 1)
                wait_bank(pe, n, p)
                cols = slice(m * P, (m + 1) * P)
                for i in range(3 * CT):
                    c, term = divmod(i, 3)
                    if kind == 2:
                        stationary = (xn_lo if term == 2 else xn_hi)[:, slot, c, cols]
                        moving = (w_lo if term == 1 else w_hi)[:, 2, c, :]
                    else:
                        stationary = (w_lo if term == 2 else w_hi)[:, kind, c, cols]
                        moving = (xn_lo if term == 1 else xn_hi)[:, slot, c, :]
                    last = nc.tensor.matmul(acc[:, p % 4, :], stationary, moving,
                                            start=(i == 0), stop=(i == 3 * CT - 1))
                last.then_inc(v_ready if kind == 2 else qk_ready, 1)

            def chunk(k, slot):
                n = 2 * k + slot
                pe.wait_ge(xn_lo_done, n + 1)
                for m in range(CT):
                    for kind in range(3):
                        group(n, slot, 3 * m + kind)
                    pe.wait_ge(sq_lo_done, 4 * n + m + 1)
                    if m == 0:
                        wait(pe, aa_lo_done, n)
                    nc.tensor.matmul(aa_ps[:, :], sel[:, m, :], sq_hi[:, m % 2, :], start=(m == 0), stop=False)
                    last = nc.tensor.matmul(aa_ps[:, :], sel[:, m, :], sq_lo[:, m % 2, :],
                                            start=False, stop=(m == CT - 1))
                    last.then_inc(sq_used, 1)

            pe.wait_ge(sel_done, 1)
            chunk(0, 0)
            with pe.Fori(0, NCH // 2 - 1, 1) as k:
                chunk(k, 1)
                chunk(k + 1, 0)
            chunk(NCH // 2 - 1, 1)


def attention(nc, ident_d, q_s, k_s, v_s, aa_s, o_s):
    with ExitStack() as ctx:
        def sb(name, shape, dt=F32):
            return ctx.enter_context(nc.sbuf_tensor(name, shape, dt))

        def sem(name):
            return ctx.enter_context(nc.semaphore(name))

        k_max = sb("p2_k_max", [D + 2, 2, N], F32R)
        k_one = sb("p2_k_one", [P, 2, N], F32R)
        k_two = sb("p2_k_two", [D + 3, 2, N], F32R)
        v_sb = sb("p2_v", [P, JT, P])
        q_max = sb("p2_q_max", [D + 2, 2, 2, CH], F32R)
        q_one = sb("p2_q_one", [P, 2, 2, CH], F32R)
        q_two = sb("p2_q_two", [D + 3, 2, 2, CH], F32R)
        probs = sb("p2_probs", [P, PSLOTS, 2, CH])
        row_max = sb("p2_row_max", [P, 2 * CH // P, NCH])
        r_col = sb("p2_r_col", [P, 2 * CH // P])
        r_row = sb("p2_r_row", [2 * CH // P, 2, P], F32R)
        den_dve = sb("p2_den_dve", [P, 2, CH])
        den_pool = sb("p2_den_pool", [P, 2, CH])
        den_sum = sb("p2_den_sum", [P, 2, CH])
        out_raw = sb("p2_out_raw", [P, CH])
        den_inv = sb("p2_den_inv", [P, CH])
        out_norm = sb("p2_out_norm", [P, 2, CH])
        ident = sb("p2_ident", [P, P])
        ones = sb("p2_ones", [P, D])
        scores = ctx.enter_context(nc.psum_tensor("p2_scores", [P, 2, 2, CH], F32))
        max_ps = ctx.enter_context(nc.psum_tensor("p2_max", [P, 2, CH], F32))
        out_ps = ctx.enter_context(nc.psum_tensor("p2_out", [P, CH], F32))
        misc_ps = ctx.enter_context(nc.psum_tensor("p2_misc", [P, CH], F32))

        consts_loaded = sem("p2_consts_loaded")
        q_max_set, q_two_set, k_two_set, ones_set = (
            sem(f"p2_{n}_set") for n in ("q_max", "q_two", "k_two", "ones"))
        km_loaded = [sem(f"p2_km_loaded{c}") for c in range(NCH)]
        kab_loaded = [sem(f"p2_kab_loaded{c}") for c in range(NCH)]
        qm_loaded = [sem(f"p2_qm_loaded{s}") for s in range(2)]
        qab_loaded = [sem(f"p2_qab_loaded{s}") for s in range(2)]
        r_loaded = [sem(f"p2_r_loaded{s}") for s in range(2)]
        max_ready = sem("p2_max_ready")
        max_read = sem("p2_max_read")
        r_ready = sem("p2_r_ready")
        r_turned = sem("p2_r_turned")
        r_copied = sem("p2_r_copied")
        scores_ready = sem("p2_scores_ready")
        probs_ready = sem("p2_probs_ready")
        probs_used = sem("p2_probs_used")
        dve_added = sem("p2_dve_added")
        pool_added = sem("p2_pool_added")
        den_summed = sem("p2_den_summed")
        den_ready = sem("p2_den_ready")
        den_inverted = sem("p2_den_inverted")
        out_copied = sem("p2_out_copied")
        normalised = sem("p2_normalised")
        out_stored = [sem(f"p2_out_stored{s}") for s in range(2)]
        block = ctx.enter_context(nc.Block())

        def dve_ops_through(jt):
            return max(DVE_JTS.index(jt), 1)

        def pool_ops_through(jt):
            return max(POOL_JTS.index(jt), 1)

        def units_of(step):
            return range(min(UNITS_PER_STEP * step, UNITS), min(UNITS_PER_STEP * (step + 1), UNITS))

        @block.sync
        def _(sp):
            sp.dma_start(ident[:, :], ident_d).then_inc(consts_loaded, 16)

            def load_k_max(pair, c):
                for h in range(2):
                    cols = slice(c * CH, (c + 1) * CH)
                    sp.dma_start(k_max[0:D, h, cols].bitcast(F32),
                                 k_s[2 * pair + h, 0, :, cols]).then_inc(km_loaded[c], 16)
                    sp.dma_start(k_max[D:D + 2, h, cols].bitcast(F32),
                                 aa_s[2 * pair + h, :, cols]).then_inc(km_loaded[c], 16)

            def load_k_and_v(pair, c):
                cols = slice(c * CH, (c + 1) * CH)
                for h in range(2):
                    head = 2 * pair + h
                    sp.dma_start(k_one[:, h, cols].bitcast(F32),
                                 k_s[head, :, :, cols].rearrange("s c n -> (s c) n")).then_inc(kab_loaded[c], 16)
                    sp.dma_start(k_two[0:D, h, cols].bitcast(F32), k_s[head, 0, :, cols]).then_inc(kab_loaded[c], 16)
                    sp.dma_start(k_two[D:D + 2, h, cols].bitcast(F32),
                                 aa_s[head, :, cols]).then_inc(kab_loaded[c], 16)
                sp.dma_start(v_sb[:, 4 * c:4 * c + 4, :],
                             v_s[pair, :, 4 * c:4 * c + 4, :]).then_inc(kab_loaded[c], 16)

            def load_q_max(pair, chunk, slot):
                for h in range(2):
                    sp.dma_start(q_max[0:D, slot, h, :].bitcast(F32),
                                 q_s[2 * pair + h, 0, :, bass.ts(chunk, CH)]).then_inc(qm_loaded[slot], 16)

            def load_q(pair, chunk, slot):
                for h in range(2):
                    head, cols = 2 * pair + h, bass.ts(chunk, CH)
                    sp.dma_start(q_one[0:D, slot, h, :].bitcast(F32),
                                 q_s[head, 0, :, cols]).then_inc(qab_loaded[slot], 16)
                    sp.dma_start(q_one[D:P, slot, h, :].bitcast(F32),
                                 q_s[head, 0, :, cols]).then_inc(qab_loaded[slot], 16)
                    sp.dma_start(q_two[0:D, slot, h, :].bitcast(F32),
                                 q_s[head, 1, :, cols]).then_inc(qab_loaded[slot], 16)

            def load_r(tile, slot):
                sp.wait_ge(r_copied, tile + 1)
                for h in range(2):
                    sp.dma_start(q_two[D + 2:D + 3, slot, h, :].rearrange("o (s n) -> o s n", n=P).bitcast(F32),
                                 r_row[4 * h:4 * h + 4, slot, :].bitcast(F32)).then_inc(r_loaded[slot], 16)

            load_q_max(0, 0, 0)
            for c in range(NCH):
                load_k_max(0, c)
            load_q(0, 0, 0)
            load_q_max(0, 1, 1)
            sp.wait_ge(k_two_set, 1)
            for c in range(NCH):
                load_k_and_v(0, c)
            sp.wait_ge(q_two_set, 1)
            load_r(0, 0)

            def queries_ahead(pair, t, slot, maxima=True):
                tile = NCH * pair + t
                sp.wait_ge(scores_ready, JT * tile + 1)
                if maxima:
                    load_q_max((tile + 2) // NCH, (tile + 2) % NCH, slot)
                load_q((tile + 1) // NCH, (tile + 1) % NCH, 1 - slot)

            def plain_tiles(pair):
                with sp.Fori(0, (NCH - 2) // 2, 1) as k:
                    for slot in range(2):
                        queries_ahead(pair, 2 * k + slot, slot)
                        load_r(NCH * pair + 2 * k + slot + 1, 1 - slot)

            with sp.Fori(0, HEADS // 2 - 1, 1) as pair:
                plain_tiles(pair)
                tile = NCH * pair + NCH - 2
                queries_ahead(pair, NCH - 2, 0)
                for c in range(NCH):
                    sp.wait_ge(max_ready, UNITS * (tile + 1) + 8 * (c + 1))
                    load_k_max(pair + 1, c)
                load_r(tile + 1, 1)
                tile = NCH * pair + NCH - 1
                queries_ahead(pair, NCH - 1, 1)
                for c in range(NCH):
                    if c == NCH - 1:
                        load_r(tile + 1, 0)
                    sp.wait_ge(scores_ready, JT * tile + 4 * (c + 1))
                    sp.wait_ge(probs_used, JT * tile + 4 * (c + 1))
                    load_k_and_v(pair + 1, c)
            plain_tiles(HEADS // 2 - 1)
            queries_ahead(HEADS // 2 - 1, NCH - 2, 0, maxima=False)
            load_r(TILES - 1, 1)

        @block.tensor
        def _(pe):
            pe.wait_ge(consts_loaded, 16)
            pe.wait_ge(ones_set, 1)
            pe.wait_ge(q_max_set, 1)

            def maximum_unit(tile, slot, u, start=False):
                c, h, s = u // 8, (u % 8) // 4, u % 4
                if u == 0:
                    pe.wait_ge(qm_loaded[slot], 16 * QM_DMAS * (tile // 2 + 1))
                if u % 8 == 0:
                    pe.wait_ge(km_loaded[c], 16 * KM_DMAS * (tile // NCH + 1))
                if not (start and u < 2):
                    pe.wait_ge(max_read, UNITS * tile + u - 1)
                nc.tensor.matmul(max_ps[:, u % 2, :], q_max[:, slot, h, s * P:(s + 1) * P],
                                 k_max[:, h, c * CH:(c + 1) * CH], start=True, stop=True).then_inc(max_ready, 1)

            def turn_maxima(tile, first=False):
                pe.wait_ge(r_ready, tile + 1)
                if not first:
                    pe.wait_ge(den_inverted, tile - 1)
                nc.tensor.matmul(misc_ps[0:2 * CH // P, 0:P], r_col[:, :], ident[:, :],
                                 start=True, stop=True).then_inc(r_turned, 1)

            def score(tile, slot, jt, h, start):
                if h == 0 and not (start and jt < 2):
                    pe.wait_ge(probs_ready, JT * tile + jt - 1)
                keys = slice(jt * P, (jt + 1) * P)
                nc.tensor.matmul(scores[:, jt % 2, h, :], k_one[:, h, keys], q_one[:, slot, h, :],
                                 start=True, stop=False)
                last = nc.tensor.matmul(scores[:, jt % 2, h, :], k_two[:, h, keys], q_two[:, slot, h, :],
                                        start=False, stop=True)
                if h == 1:
                    last.then_inc(scores_ready, 1)

            def times_v(tile, jt):
                pe.wait_ge(probs_ready, JT * tile + jt + 1)
                for h in range(2):
                    last = nc.tensor.matmul(out_ps[h * D:(h + 1) * D, :], v_sb[:, jt, h * D:(h + 1) * D],
                                            probs[:, jt % PSLOTS, h, :], start=(jt == 0), stop=(jt == JT - 1))
                last.then_inc(probs_used, 1)

            def denominators(tile):
                pe.wait_ge(den_summed, tile + 1)
                pe.wait_ge(r_copied, tile + 2 if tile is not TILES - 1 else TILES)
                for h in range(2):
                    last = nc.tensor.matmul(misc_ps[h * D:(h + 1) * D, :], ones[:, :], den_sum[:, h, :],
                                            start=True, stop=True)
                last.then_inc(den_ready, 1)

            def attend(tile, slot, start=False, maxima=True):
                pe.wait_ge(qab_loaded[slot], 16 * QAB_DMAS * (tile // 2 + 1))
                pe.wait_ge(r_loaded[slot], 32 * (tile // 2 + 1))
                for step in range(JT // 2):
                    if step % 2 == 0:
                        pe.wait_ge(kab_loaded[step // 2], 16 * KAB_DMAS * (tile // NCH + 1))
                    units = units_of(step) if maxima else ()
                    for i in range(4):
                        score(tile, slot, 2 * step + i // 2, i % 2, start)
                        for u in units[i:i + 1]:
                            maximum_unit(tile + 1, 1 - slot, u)
                    if step == 0 and not start:
                        for jt in (JT - 2, JT - 1):
                            times_v(tile - 1, jt)
                    if step == 1 and not start:
                        pe.wait_ge(out_copied, tile)
                    if step >= 1:
                        for jt in (2 * step - 2, 2 * step - 1):
                            times_v(tile, jt)
                    for u in units[4:]:
                        maximum_unit(tile + 1, 1 - slot, u)
                    if step == 3 and not start:
                        denominators(tile - 1)
                    if step == JT // 2 - 2 and maxima:
                        turn_maxima(tile + 1)

            for u in range(UNITS):
                maximum_unit(0, 0, u, start=True)
            turn_maxima(0, first=True)
            attend(0, 0, start=True)
            attend(1, 1)
            attend(2, 0)
            with pe.Fori(0, (TILES - 4) // 2, 1) as k:
                attend(2 * k + 3, 1)
                attend(2 * k + 4, 0)
            attend(TILES - 1, 1, maxima=False)
            for jt in (JT - 2, JT - 1):
                times_v(TILES - 1, jt)
            denominators(TILES - 1)

        @block.scalar
        def _(act):
            def exponentials(tile, jt, start):
                act.wait_ge(scores_ready, JT * tile + jt + 1)
                if not (start and jt < PSLOTS):
                    act.wait_ge(probs_used, JT * tile + jt - PSLOTS + 1)
                    before = tile if jt >= PSLOTS else tile - 1
                    j = (jt - PSLOTS) % JT
                    if j in POOL_JTS:
                        act.wait_ge(pool_added, POOL_OPS * before + pool_ops_through(j))
                    else:
                        act.wait_ge(dve_added, DVE_OPS * before + dve_ops_through(j))
                nc.scalar.activation(probs[:, jt % PSLOTS, :, :], scores[:, jt % 2, :, :], ACT.Exp,
                                     scale=0.25).then_inc(probs_ready, 1)

            def copy_out(tile, first=False):
                act.wait_ge(probs_used, JT * (tile + 1))
                if not first:
                    act.wait_ge(normalised, tile)
                nc.scalar.copy(out_raw[:, :], out_ps[:, :]).then_inc(out_copied, 1)

            def store(tile, slot):
                act.wait_ge(normalised, tile + 1)
                act.dma_start(o_s[tile, :, :], out_norm[:, slot, :]).then_inc(out_stored[slot], 16)

            def attend(tile, slot, start=False, second=False):
                for jt in range(JT):
                    exponentials(tile, jt, start)
                    if jt == 1 and not start:
                        copy_out(tile - 1)
                    if jt == JT - 1 and not start:
                        store(tile - 1, 1 - slot)

            attend(0, 0, start=True)
            attend(1, 1)
            attend(2, 0)
            with act.Fori(0, (TILES - 4) // 2, 1) as k:
                attend(2 * k + 3, 1)
                attend(2 * k + 4, 0)
            attend(TILES - 1, 1)
            copy_out(TILES - 1)
            store(TILES - 1, 1)
            for s in range(2):
                act.wait_ge(out_stored[s], 16 * TILES // 2)

        @block.vector
        def _(dve):
            nc.vector.memset(q_max[D:D + 2, :, :, :].bitcast(F32), 1.0).then_inc(q_max_set, 1)
            nc.vector.memset(ones[:, :], 1.0).then_inc(ones_set, 1)

            def maximum_unit(tile, u, first=False):
                c, h, s = u // 8, (u % 8) // 4, u % 4
                if u == 0 and not first:
                    dve.wait_ge(r_ready, tile)
                dve.wait_ge(max_ready, UNITS * tile + u + 1)
                nc.vector.tensor_reduce(row_max[:, 4 * h + s, c:c + 1], max_ps[:, u % 2, :], AX.X,
                                        ALU.max).then_inc(max_read, 1)

            def row_maxima(tile, first=False):
                dve.wait_ge(max_read, UNITS * (tile + 1))
                if not first:
                    dve.wait_ge(r_turned, tile)
                nc.vector.tensor_reduce(r_col[:, :], row_max[:, :, :], AX.X, ALU.max).then_inc(r_ready, 1)

            def copy_maxima(tile, half):
                slot = half[1]
                dve.wait_ge(r_turned, tile + 1)
                dve.wait_ge(r_loaded[slot], 32 * half[0])
                nc.vector.tensor_scalar(r_row[:, slot, :], misc_ps[0:2 * CH // P, 0:P], -1.0, None,
                                        ALU.mult).then_inc(r_copied, 1)

            def add(tile, jt):
                if jt not in DVE_JTS[1:]:
                    return
                k = DVE_JTS.index(jt)
                dve.wait_ge(probs_ready, JT * tile + jt + 1)
                dve.wait_ge(dve_added, DVE_OPS * tile + k - 1)
                before = probs[:, DVE_JTS[0], :, :] if k == 1 else den_dve[:, :, :]
                nc.vector.tensor_tensor(den_dve[:, :, :], before, probs[:, jt % PSLOTS, :, :],
                                        ALU.add).then_inc(dve_added, 1)

            def sum_denominators(tile):
                dve.wait_ge(dve_added, DVE_OPS * (tile + 1))
                dve.wait_ge(pool_added, POOL_OPS * (tile + 1))
                dve.wait_ge(den_ready, tile)
                nc.vector.tensor_tensor(den_sum[:, :, :], den_dve[:, :, :], den_pool[:, :, :],
                                        ALU.add).then_inc(den_summed, 1)
                dve.wait_ge(den_summed, tile + 1)

            def normalise(tile, half):
                slot = half[1]
                dve.wait_ge(den_ready, tile + 1)
                dve.wait_ge(normalised, tile)
                nc.vector.reciprocal(den_inv[:, :], misc_ps[:, :]).then_inc(den_inverted, 1)
                dve.wait_ge(den_inverted, tile + 1)
                dve.wait_ge(out_copied, tile + 1)
                dve.wait_ge(out_stored[slot], 16 * half[0])
                nc.vector.tensor_tensor(out_norm[:, slot, :], out_raw[:, :], den_inv[:, :],
                                        ALU.mult).then_inc(normalised, 1)

            def attend(k, slot, start=False, maxima=True):
                tile = 2 * k + slot
                before = (k, 0) if slot else (k - 1, 1)
                after = (k + 1, 0) if slot else (k, 1)
                for step in range(JT // 2):
                    units = units_of(step) if maxima else ()
                    for u in units[:4]:
                        maximum_unit(tile + 1, u)
                    if step == 0 and not start:
                        for jt in (JT - 2, JT - 1):
                            add(tile - 1, jt)
                    if step == 1 and not start:
                        sum_denominators(tile - 1)
                    if step >= 1:
                        for jt in (2 * step - 2, 2 * step - 1):
                            add(tile, jt)
                    for u in units[4:]:
                        maximum_unit(tile + 1, u)
                    if UNITS - 1 in units:
                        row_maxima(tile + 1)
                    if step == JT // 2 - 3 and not start:
                        normalise(tile - 1, before)
                    if step == JT // 2 - 1 and maxima:
                        copy_maxima(tile + 1, after)

            for u in range(UNITS):
                maximum_unit(0, u, first=True)
            row_maxima(0, first=True)
            copy_maxima(0, (0, 0))
            attend(0, 0, start=True)
            attend(0, 1)
            attend(1, 0)
            with dve.Fori(0, (TILES - 4) // 2, 1) as k:
                attend(k + 1, 1)
                attend(k + 2, 0)
            attend(TILES // 2 - 1, 1, maxima=False)
            for jt in (JT - 2, JT - 1):
                add(TILES - 1, jt)
            sum_denominators(TILES - 1)
            normalise(TILES - 1, (TILES // 2 - 1, 1))

        @block.gpsimd
        def _(pool):
            nc.gpsimd.memset(q_two[D:D + 3, :, :, :].bitcast(F32), 1.0).then_inc(q_two_set, 1)
            nc.gpsimd.memset(k_two[D:D + 3, :, :].bitcast(F32), 1.0).then_inc(k_two_set, 1)

            def add_up(tile):
                for k, jt in enumerate(POOL_JTS[1:], 1):
                    pool.wait_ge(probs_ready, JT * tile + jt + 1)
                    pool.wait_ge(pool_added, POOL_OPS * tile + k - 1)
                    if k == 1:
                        pool.wait_ge(den_summed, tile)
                    before = probs[:, POOL_JTS[0], :, :] if k == 1 else den_pool[:, :, :]
                    nc.gpsimd.tensor_tensor(den_pool[:, :, :], before, probs[:, jt % PSLOTS, :, :],
                                            ALU.add).then_inc(pool_added, 1)

            add_up(0)
            with pool.Fori(0, TILES - 1, 1) as k:
                add_up(k + 1)


def output_and_convolution(nc, x, wo_t, gmat_d, taps_d, o_s, z):
    with ExitStack() as ctx:
        def sb(name, shape, dt=F32):
            return ctx.enter_context(nc.sbuf_tensor(name, shape, dt))

        def sem(name):
            return ctx.enter_context(nc.semaphore(name))

        y_sb = sb("p3_y", [P, CT, N])
        w_raw = sb("p3_w_raw", [P, CT, C])
        w_hi = sb("p3_w_hi", [P, CT, C], F32R)
        w_lo = sb("p3_w_lo", [P, CT, C], F32R)
        o_raw = sb("p3_o_raw", [P, 2, CT, CH])
        o_hi = sb("p3_o_hi", [P, 2, CT, CH], F32R)
        o_lo = sb("p3_o_lo", [P, 2, CT, CH], F32R)
        x_res = sb("p3_x_res", [P, 2, CT, CH])
        gmat = sb("p3_gmat", [P, P])
        taps = sb("p3_taps", [P, 3 * P])
        taps_hi = sb("p3_taps_hi", [P, 3 * P], F32R)
        taps_lo = sb("p3_taps_lo", [P, 3 * P], F32R)
        stats = sb("p3_stats", [P, CT, NCH, 6])
        mv = sb("p3_mv", [P, CT, 2])
        ex = sb("p3_ex", [P, CT, 2])
        root = sb("p3_root", [P, CT, 2])
        mean = sb("p3_mean", [P, CT])
        rstd = sb("p3_rstd", [P, CT])
        acc = ctx.enter_context(nc.psum_tensor("p3_acc", [P, CT, CH], F32))
        gn_ps = ctx.enter_context(nc.psum_tensor("p3_gn", [P, CT, 2], F32))
        yn, yn_hi, yn_lo, z_st = o_raw, o_hi, o_lo, x_res

        consts_loaded = sem("p3_consts_loaded")
        w_loaded = sem("p3_w_loaded")
        w_hi_done = sem("p3_w_hi_done")
        w_lo_done = sem("p3_w_lo_done")
        o_loaded = [sem(f"p3_o_loaded{s}") for s in range(2)]
        x_loaded = [sem(f"p3_x_loaded{s}") for s in range(2)]
        o_hi_done = sem("p3_o_hi_done")
        o_lo_done = sem("p3_o_lo_done")
        wo_ready = sem("p3_wo_ready")
        y_done = sem("p3_y_done")
        stats_done = sem("p3_stats_done")
        gn_ready = sem("p3_gn_ready")
        taps_hi_done = sem("p3_taps_hi_done")
        taps_lo_done = sem("p3_taps_lo_done")
        yn_done = sem("p3_yn_done")
        yn_hi_done = sem("p3_yn_hi_done")
        yn_lo_done = sem("p3_yn_lo_done")
        conv_ready = sem("p3_conv_ready")
        z_done = sem("p3_z_done")
        z_stored = [sem(f"p3_z_stored{s}") for s in range(2)]
        gn_vector, gn_tensor, gn_scalar = group_statistics(
            nc, lambda n: sem("p3_" + n), stats, mv, ex, gn_ps, gmat, root, mean, rstd, gn_ready)
        block = ctx.enter_context(nc.Block())

        @block.sync
        def _(sp):
            def load(n, slot):
                sp.dma_start(o_raw[:, slot, :, :],
                             o_s.rearrange("(q t) p n -> t p q n", t=NCH)[n, :, :, :]).then_inc(o_loaded[slot], 16)
                sp.dma_start(x_res[:, slot, :, :],
                             x[:, bass.ts(n, CH)].rearrange("(m p) n -> p m n", p=P)).then_inc(x_loaded[slot], 16)

            load(0, 0)
            load(1, 1)
            sp.dma_start(gmat[:, :], gmat_d).then_inc(consts_loaded, 16)
            sp.dma_start(taps[:, :], bass.AP(tensor=taps_d.tensor, offset=P - 1,
                                             ap=[[C - 1, P], [1, 3 * P]])).then_inc(consts_loaded, 16)
            with sp.Fori(0, (NCH - 2) // 2, 1) as k:
                for slot in range(2):
                    sp.wait_ge(y_done, CT * (2 * k + slot + 1))
                    sp.wait_ge(o_lo_done, 2 * k + slot + 1)
                    load(2 * k + slot + 2, slot)
            with sp.Fori(0, NCH // 2, 1) as k:
                for slot in range(2):
                    sp.wait_ge(z_done, CT * (2 * k + slot + 1))
                    sp.dma_start(z[:, bass.ts(2 * k + slot, CH)].rearrange("(m p) n -> p m n", p=P),
                                 z_st[:, slot, :, :]).then_inc(z_stored[slot], 16)
            for s in range(2):
                sp.wait_ge(z_stored[s], 16 * NCH // 2)

        @block.scalar
        def _(act):
            act.dma_start(w_raw[:, :, :], wo_t.rearrange("(m p) o -> p m o", p=P)).then_inc(w_loaded, 16)
            act.wait_ge(w_loaded, 16)
            nc.scalar.copy(w_hi[:, :, :], w_raw[:, :, :]).then_inc(w_hi_done, 1)

            def split(k, slot):
                act.wait_ge(o_loaded[slot], 16 * (k + 1))
                wait(act, wo_ready, CT * (2 * k + slot - 1))
                nc.scalar.copy(o_hi[:, slot, :, :], o_raw[:, slot, :, :]).then_inc(o_hi_done, 1)

            split(0, 0)
            split(0, 1)
            with act.Fori(0, NCH // 2 - 1, 1) as k:
                split(k + 1, 0)
                split(k + 1, 1)
            gn_scalar(act)
            act.wait_ge(consts_loaded, 32)
            nc.scalar.copy(taps_hi[:, :], taps[:, :]).then_inc(taps_hi_done, 1)

            def normalised_hi(k, slot):
                n = 2 * k + slot
                act.wait_ge(yn_done, CT * (n + 1))
                wait(act, conv_ready, CT * (n - 1))
                if isinstance(n, int) and n < 2:
                    act.wait_ge(wo_ready, CT * NCH)
                nc.scalar.copy(yn_hi[:, slot, :, :], yn[:, slot, :, :]).then_inc(yn_hi_done, 1)

            normalised_hi(0, 0)
            normalised_hi(0, 1)
            with act.Fori(0, NCH // 2 - 1, 1) as k:
                normalised_hi(k + 1, 0)
                normalised_hi(k + 1, 1)

        @block.vector
        def _(dve):
            dve.wait_ge(w_hi_done, 1)
            nc.vector.tensor_tensor(w_lo[:, :, :], w_raw[:, :, :], w_hi[:, :, :].bitcast(F32),
                                    ALU.subtract).then_inc(w_lo_done, 1)

            def split(n, slot):
                dve.wait_ge(o_hi_done, n + 1)
                nc.vector.tensor_tensor(o_lo[:, slot, :, :], o_raw[:, slot, :, :],
                                        o_hi[:, slot, :, :].bitcast(F32), ALU.subtract).then_inc(o_lo_done, 1)

            def residual(n, k, slot):
                dve.wait_ge(x_loaded[slot], 16 * (k + 1))
                for m in range(CT):
                    dve.wait_ge(wo_ready, CT * n + m + 1)
                    nc.vector.scalar_tensor_tensor(
                        out=y_sb[:, m, bass.ts(n, CH)], in0=acc[:, m, :], scalar=GAIN,
                        in1=x_res[:, slot, m, :], op0=ALU.mult, op1=ALU.add).then_inc(y_done, 1)
                dve.wait_ge(y_done, CT * (n + 1))
                for m in range(CT):
                    nc.vector.bn_stats(stats[:, m, n, :], y_sb[:, m, bass.ts(n, CH)]).then_inc(stats_done, 1)

            split(0, 0)
            with dve.Fori(0, NCH // 2 - 1, 1) as k:
                split(2 * k + 1, 1)
                residual(2 * k, k, 0)
                split(2 * k + 2, 0)
                residual(2 * k + 1, k, 1)
            split(NCH - 1, 1)
            residual(NCH - 2, NCH // 2 - 1, 0)
            residual(NCH - 1, NCH // 2 - 1, 1)
            dve.wait_ge(stats_done, CT * NCH)
            gn_vector(dve)

            dve.wait_ge(taps_hi_done, 1)
            nc.vector.tensor_tensor(taps_lo[:, :], taps[:, :], taps_hi[:, :].bitcast(F32),
                                    ALU.subtract).then_inc(taps_lo_done, 1)

            def normalise(k, slot):
                n = 2 * k + slot
                wait(dve, yn_lo_done, n - 1)
                for m in range(CT):
                    nc.vector.tensor_scalar(yn[:, slot, m, :], y_sb[:, m, bass.ts(n, CH)], mean[:, m:m + 1],
                                            rstd[:, m:m + 1], ALU.subtract, ALU.mult).then_inc(yn_done, 1)

            def normalised_lo(k, slot):
                dve.wait_ge(yn_hi_done, 2 * k + slot + 1)
                dve.wait_ge(yn_done, CT * (2 * k + slot + 1))
                nc.vector.tensor_tensor(yn_lo[:, slot, :, :], yn[:, slot, :, :],
                                        yn_hi[:, slot, :, :].bitcast(F32), ALU.subtract).then_inc(yn_lo_done, 1)

            def finish(k, slot):
                wait(dve, z_stored[slot], 16 * k)
                for m in range(CT):
                    dve.wait_ge(conv_ready, CT * (2 * k + slot) + m + 1)
                    nc.vector.tensor_tensor(z_st[:, slot, m, :], acc[:, m, :],
                                            y_sb[:, m, bass.ts(2 * k + slot, CH)], ALU.add).then_inc(z_done, 1)

            normalise(0, 0)
            normalise(0, 1)
            normalised_lo(0, 0)
            normalised_lo(0, 1)

            def follow(k, slot):
                normalise(k + 1, slot)
                finish(k, slot)
                normalised_lo(k + 1, slot)

            follow(0, 0)
            follow(0, 1)
            with dve.Fori(0, NCH // 2 - 2, 1) as k:
                follow(k + 1, 0)
                follow(k + 1, 1)
            finish(NCH // 2 - 1, 0)
            finish(NCH // 2 - 1, 1)

        @block.tensor
        def _(pe):
            def project(k, slot):
                pe.wait_ge(o_lo_done, 2 * k + slot + 1)
                for m in range(CT):
                    wait(pe, y_done, 8 * k + (m + 1 if slot else 0))
                    cols = slice(m * P, (m + 1) * P)
                    for i in range(3 * CT):
                        c, term = divmod(i, 3)
                        last = nc.tensor.matmul(acc[:, m, :],
                                                (w_lo if term == 2 else w_hi)[:, c, cols],
                                                (o_lo if term == 1 else o_hi)[:, slot, c, :],
                                                start=(i == 0), stop=(i == 3 * CT - 1))
                    last.then_inc(wo_ready, 1)

            def convolve(k, slot):
                pe.wait_ge(yn_lo_done, 2 * k + slot + 1)
                for m in range(CT):
                    wait(pe, z_done, 8 * k + (m + 1 if slot else 0))
                    for i in range(9):
                        source, term = divmod(i, 3)
                        cols = slice((2 - source) * P, (3 - source) * P)
                        last = nc.tensor.matmul(acc[:, m, :], (taps_lo if term == 2 else taps_hi)[:, cols],
                                                (yn_lo if term == 1 else yn_hi)[:, slot, (m + source - 1) % CT, :],
                                                start=(i == 0), stop=(i == 8))
                    last.then_inc(conv_ready, 1)

            pe.wait_ge(w_lo_done, 1)
            project(0, 0)
            project(0, 1)
            with pe.Fori(0, NCH // 2 - 1, 1) as k:
                project(k + 1, 0)
                project(k + 1, 1)
            pe.wait_ge(consts_loaded, 32)
            gn_tensor(pe)
            pe.wait_ge(y_done, CT * NCH)
            pe.wait_ge(taps_lo_done, 1)
            convolve(0, 0)
            convolve(0, 1)
            with pe.Fori(0, NCH // 2 - 1, 1) as k:
                convolve(k + 1, 0)
                convolve(k + 1, 1)


def build(nc, x, wq_t, wk_t, wv_t, wo_t, taps, gmat, sel, ident, z):
    q_s = nc.dram_tensor("q_scratch", [HEADS, 2, D, N], F32, kind="Internal").ap()
    k_s = nc.dram_tensor("k_scratch", [HEADS, 2, D, N], F32, kind="Internal").ap()
    v_s = nc.dram_tensor("v_scratch", [HEADS // 2, P, JT, P], F32, kind="Internal").ap()
    aa_s = nc.dram_tensor("aa_scratch", [HEADS, 2, N], F32, kind="Internal").ap()
    o_s = nc.dram_tensor("o_scratch", [TILES, P, CH], F32, kind="Internal").ap()
    projections(nc, x, wq_t, wk_t, wv_t, gmat, sel, q_s, k_s, v_s, aa_s)
    attention(nc, ident, q_s, k_s, v_s, aa_s, o_s)
    output_and_convolution(nc, x, wo_t, gmat, taps, o_s, z)


def kernel(x, L0_conv_wq, L0_conv_wk, L0_conv_wv, L0_conv_wo, L1_conv_inhibition_filter):
    import numpy as np
    import concourse.bacc as bacc
    from concourse.bass_utils import run_bass_kernel_spmd

    left = (C - SCOPE) // 2
    padded = np.pad(np.asarray(L1_conv_inhibition_filter)[0, 0], (left, C - SCOPE - left))
    channel = np.arange(P)
    arrays = {
        "x_in": np.ascontiguousarray(np.asarray(x).reshape(C, N)),
        "wq_t": np.ascontiguousarray(np.asarray(L0_conv_wq).T),
        "wk_t": np.ascontiguousarray(np.asarray(L0_conv_wk).T),
        "wv_t": np.ascontiguousarray(np.asarray(L0_conv_wv).T),
        "wo_t": np.ascontiguousarray(np.asarray(L0_conv_wo).T),
        "taps": np.ascontiguousarray(np.broadcast_to(padded, (P, C))),
        "gmat": (channel[:, None] // 16 == channel[None, :] // 16).astype(np.float32) / 16,
        "sel": np.where(2 * np.arange(CT)[None, :, None] + channel[:, None, None] // D == channel,
                        -0.5, 0.0).astype(np.float32),
        "ident": np.eye(P, dtype=np.float32),
    }
    nc = bacc.Bacc("TRN2", target_bir_lowering=False, num_devices=1)
    args = [nc.dram_tensor(k, a.shape, F32, kind="ExternalInput").ap() for k, a in arrays.items()]
    z = nc.dram_tensor("z_out", (C, N), F32, kind="ExternalOutput").ap()
    build(nc, *args, z)
    r = run_bass_kernel_spmd(nc, [arrays], core_ids=[0])
    return r.results[0]["z_out"].reshape(1, C, 64, 64)
```

```python
from contextlib import ExitStack

import concourse.bass as bass
from concourse import mybir

F32 = mybir.dt.float32
F32R = mybir.dt.float32r
ALU = mybir.AluOpType
ACT = mybir.ActivationFunctionType
AX = mybir.AxisListType

C = 512
N = 4096
HEADS = 8
D = C // HEADS
P = 128
CT = C // P
CH = 512
NCH = N // CH
GAIN = float(C) ** -0.5
SCOPE = 63
REACH = SCOPE // 2
GN_EPS = 1e-5

TILES = (HEADS // 2) * NCH
JT = N // P
UNITS = 2 * (CH // P) * NCH
STEP = 4
STEPS = JT // STEP
UNITS_OF_STEPS = (8, 8, 8, 9, 9, 9, 9, 4)
PSLOTS = 8
POOL_SLOTS = (1, 2, 3, 5, 6, 7)
DVE_JTS = [j for j in range(JT) if j % PSLOTS not in POOL_SLOTS]
POOL_JTS = [j for j in range(JT) if j % PSLOTS in POOL_SLOTS]
DVE_OPS = len(DVE_JTS) - 1
POOL_OPS = len(POOL_JTS) - 1
KM_DMAS, KAB_DMAS, QM_DMAS, QAB_DMAS = 4, 7, 2, 6


def wait(engine, semaphore, count):
    if not isinstance(count, int) or count > 0:
        engine.wait_ge(semaphore, count)


def group_statistics(nc, sem, stats, mv, ex, psum, gmat, root, mean, rstd, ready):
    step = sem("gn_step")
    sums = sem("gn_sums")
    rooted = sem("gn_root")

    def vector(dve):
        for m in range(CT):
            nc.vector.bn_aggr(mv[:, m, :], stats[:, m, :, :]).then_inc(step, 1)
        dve.wait_ge(step, CT)
        nc.vector.tensor_tensor(ex[:, :, 0], mv[:, :, 0], mv[:, :, 0], ALU.mult).then_inc(step, 1)
        dve.wait_ge(step, CT + 1)
        nc.vector.tensor_tensor(mv[:, :, 1], mv[:, :, 1], ex[:, :, 0], ALU.add).then_inc(step, 1)
        dve.wait_ge(sums, 1)
        nc.vector.tensor_copy(mean[:, :], psum[:, :, 0]).then_inc(step, 1)
        dve.wait_ge(step, CT + 3)
        nc.vector.tensor_tensor(ex[:, :, 0], mean[:, :], mean[:, :], ALU.mult).then_inc(step, 1)
        dve.wait_ge(step, CT + 4)
        nc.vector.tensor_tensor(ex[:, :, 1], psum[:, :, 1], ex[:, :, 0], ALU.subtract).then_inc(step, 1)
        dve.wait_ge(step, CT + 5)
        nc.vector.tensor_scalar(root[:, :, 0], ex[:, :, 1], GN_EPS, None, ALU.add).then_inc(step, 1)
        dve.wait_ge(rooted, 1)
        nc.vector.reciprocal(ex[:, :, 0], root[:, :, 1]).then_inc(step, 1)
        dve.wait_ge(step, CT + 7)
        nc.vector.tensor_tensor(ex[:, :, 1], root[:, :, 0], ex[:, :, 0], ALU.mult).then_inc(step, 1)
        dve.wait_ge(step, CT + 8)
        nc.vector.tensor_tensor(ex[:, :, 0], ex[:, :, 1], root[:, :, 1], ALU.add).then_inc(step, 1)
        dve.wait_ge(step, CT + 9)
        nc.vector.tensor_scalar(ex[:, :, 1], ex[:, :, 0], 0.5, None, ALU.mult).then_inc(step, 1)
        dve.wait_ge(step, CT + 10)
        nc.vector.reciprocal(rstd[:, :], ex[:, :, 1]).then_inc(ready, 1)
        dve.wait_ge(ready, 1)

    def tensor(pe):
        pe.wait_ge(step, CT + 2)
        nc.tensor.matmul(psum[:, :, :].rearrange("p m s -> p (m s)"), gmat[:, :],
                         mv[:, :, :].rearrange("p m s -> p (m s)"), start=True, stop=True).then_inc(sums, 1)

    def scalar(act):
        act.wait_ge(step, CT + 6)
        nc.scalar.activation(root[:, :, 1], root[:, :, 0], ACT.Sqrt).then_inc(rooted, 1)

    return vector, tensor, scalar


def projections(nc, x, wq_t, wk_t, wv_t, gmat_d, sel_d, q_s, k_s, v_s, aa_s):
    with ExitStack() as ctx:
        def sb(name, shape, dt=F32):
            return ctx.enter_context(nc.sbuf_tensor(name, shape, dt))

        def sem(name):
            return ctx.enter_context(nc.semaphore(name))

        x_sb = sb("p1_x", [P, CT, N])
        w_hi = sb("p1_w_hi", [P, 3, CT, C], F32R)
        w_lo = sb("p1_w_lo", [P, 3, CT, C], F32R)
        w_raw = sb("p1_w_raw", [P, 2, CT, C])
        xn = sb("p1_xn", [P, CT, CH])
        xn_hi = sb("p1_xn_hi", [P, 2, CT, CH], F32R)
        xn_lo = sb("p1_xn_lo", [P, 2, CT, CH], F32R)
        qk_st = sb("p1_qk_st", [P, 2, 2, CH], F32R)
        v_and_sq = sb("p1_v_and_sq", [P, 4, CH])
        v_st, sq = v_and_sq[:, 0:2, :], v_and_sq[:, 2:4, :]
        sq_hi = sb("p1_sq_hi", [P, 2, CH], F32R)
        sq_lo = sb("p1_sq_lo", [P, 2, CH], F32R)
        aa_st = sb("p1_aa_st", [HEADS, 2, 2, CH], F32R)
        gmat = sb("p1_gmat", [P, P])
        sel_raw = sb("p1_sel_raw", [P, CT, P])
        sel = sb("p1_sel", [P, CT, P], F32R)
        stats = sb("p1_stats", [P, CT, NCH, 6])
        mv = sb("p1_mv", [P, CT, 2])
        ex = sb("p1_ex", [P, CT, 2])
        root = sb("p1_root", [P, CT, 2])
        mean = sb("p1_mean", [P, CT])
        rstd = sb("p1_rstd", [P, CT])
        acc = ctx.enter_context(nc.psum_tensor("p1_acc", [P, 4, CH], F32))
        aa_ps = ctx.enter_context(nc.psum_tensor("p1_aa", [P, CH], F32))
        gn_ps = ctx.enter_context(nc.psum_tensor("p1_gn", [P, CT, 2], F32))

        x_loaded = [[sem(f"p1_x_loaded{m}{half}") for half in "ab"] for m in range(CT)]
        consts_loaded = sem("p1_consts_loaded")
        w_loaded = [sem(f"p1_w_loaded{w}") for w in range(3)]
        sel_done = sem("p1_sel_done")
        w_hi_done = sem("p1_w_hi_done")
        w_lo_done = [sem(f"p1_w_lo_done{w}") for w in range(3)]
        stats_done = sem("p1_stats_done")
        gn_ready = sem("p1_gn_ready")
        xn_done = sem("p1_xn_done")
        xn_hi_done = sem("p1_xn_hi_done")
        xn_lo_done = sem("p1_xn_lo_done")
        qk_ready = sem("p1_qk_ready")
        v_ready = sem("p1_v_ready")
        sq_used = sem("p1_sq_used")
        qk_hi_done = sem("p1_qk_hi_done")
        qk_lo_done = sem("p1_qk_lo_done")
        sq_done = sem("p1_sq_done")
        sq_lo_done = sem("p1_sq_lo_done")
        v_done = sem("p1_v_done")
        aa_hi_done = sem("p1_aa_hi_done")
        aa_lo_done = sem("p1_aa_lo_done")
        qk_stored = [sem(f"p1_qk_stored{s}") for s in range(2)]
        v_stored = [sem(f"p1_v_stored{s}") for s in range(2)]
        aa_stored = [sem(f"p1_aa_stored{s}") for s in range(2)]
        gn_vector, gn_tensor, gn_scalar = group_statistics(
            nc, lambda n: sem("p1_" + n), stats, mv, ex, gn_ps, gmat, root, mean, rstd, gn_ready)
        block = ctx.enter_context(nc.Block())
        weights = (wq_t, wk_t, wv_t)
        raw = (w_raw[:, 0, :, :], w_raw[:, 1, :, :], v_and_sq[:, :, :])

        def wait_bank(pe, n, p):
            m, kind = divmod((p - 4) % 12, 3)
            before = n if p >= 4 else n - 1
            if kind == 2:
                wait(pe, v_done, 4 * before + m + 1)
            else:
                wait(pe, qk_lo_done, 8 * before + 2 * m + kind + 1)

        @block.sync
        def _(sp):
            sp.dma_start(gmat[:, :], gmat_d).then_inc(consts_loaded, 16)
            sp.dma_start(sel_raw[:, :, :], sel_d).then_inc(consts_loaded, 16)
            for m in range(CT):
                for half in range(2):
                    cols = slice(half * N // 2, (half + 1) * N // 2)
                    sp.dma_start(x_sb[:, m, cols], x[m * P:(m + 1) * P, cols]).then_inc(x_loaded[m][half], 16)
            for w in range(3):
                sp.dma_start(raw[w], weights[w].rearrange("(c p) o -> p c o", p=P)).then_inc(w_loaded[w], 16)
            def store(k, slot):
                n = 2 * k + slot
                for m in range(CT):
                    for kind, dst in enumerate((q_s, k_s)):
                        sp.wait_ge(qk_lo_done, 8 * n + 2 * m + kind + 1)
                        for h in range(2):
                            sp.dma_start(dst[2 * m + h, :, :, bass.ts(n, CH)].rearrange("s c n -> c s n"),
                                         qk_st[h * D:(h + 1) * D, kind, :, :].bitcast(F32)
                                         ).then_inc(qk_stored[kind], 16)
                    sp.wait_ge(v_done, 4 * n + m + 1)
                    sp.dma_start(v_s[:, :, 4 * n + m, :].rearrange("q p d -> p q d"),
                                 v_st[:, m % 2, :].rearrange("p (q d) -> p q d", q=CT)
                                 ).then_inc(v_stored[m % 2], 16)
                sp.wait_ge(aa_lo_done, n + 1)
                sp.dma_start(aa_s[:, :, bass.ts(n, CH)], aa_st[:, slot, :, :].bitcast(F32)).then_inc(aa_stored[slot], 16)

            with sp.Fori(0, NCH // 2, 1) as k:
                store(k, 0)
                store(k, 1)
            for s in range(2):
                sp.wait_ge(qk_stored[s], 32 * CT * NCH)
                sp.wait_ge(v_stored[s], 16 * CT * NCH // 2)
                sp.wait_ge(aa_stored[s], 16 * NCH // 2)

        @block.scalar
        def _(act):
            act.wait_ge(consts_loaded, 32)
            nc.scalar.copy(sel[:, :, :], sel_raw[:, :, :]).then_inc(sel_done, 1)

            def weight_hi(w):
                act.wait_ge(w_loaded[w], 16)
                nc.scalar.copy(w_hi[:, w, :, :], raw[w]).then_inc(w_hi_done, 1)

            def normalised_hi(n, slot):
                wait(act, qk_ready, 8 * (n - 1))
                wait(act, v_ready, 4 * (n - 1))
                for m in range(CT):
                    act.wait_ge(xn_done, CT * n + m + 1)
                    nc.scalar.copy(xn_hi[:, slot, m, :], xn[:, m, :]).then_inc(xn_hi_done, 1)

            def evacuate(k, slot, prepare=True):
                n = 2 * k + slot
                for m in range(CT):
                    for kind in range(2):
                        p = 3 * m + kind
                        act.wait_ge(qk_ready, 8 * n + 2 * m + kind + 1)
                        wait(act, qk_stored[kind], 32 * (4 * n + m))
                        nc.scalar.mul(qk_st[:, kind, 0, :], acc[:, p % 4, :], GAIN).then_inc(qk_hi_done, 1)
                        if kind == 0:
                            wait(act, sq_lo_done, 4 * n + m - 1)
                            wait(act, sq_used, 4 * n + m - 1)
                            for part in (sq, sq_hi):
                                nc.scalar.activation(part[:, m % 2, :], acc[:, p % 4, :], ACT.Square,
                                                     scale=GAIN).then_inc(sq_done, 1)
                    act.wait_ge(v_ready, 4 * n + m + 1)
                    wait(act, v_stored[m % 2], 16 * (2 * n + m // 2))
                    nc.scalar.mul(v_st[:, m % 2, :], acc[:, (3 * m + 2) % 4, :], GAIN).then_inc(v_done, 1)
                    if m == 1 and prepare:
                        normalised_hi(n + 1, 1 - slot)
                act.wait_ge(sq_used, 4 * (n + 1))
                wait(act, aa_stored[slot], 16 * k)
                nc.scalar.copy(aa_st[:, slot, 0, :], aa_ps[0:HEADS, :]).then_inc(aa_hi_done, 1)

            weight_hi(0)
            gn_scalar(act)
            normalised_hi(0, 0)
            weight_hi(1)
            weight_hi(2)
            normalised_hi(1, 1)
            act.wait_ge(w_lo_done[2], 1)
            evacuate(0, 0, prepare=False)
            evacuate(0, 1)
            evacuate(1, 0)
            with act.Fori(0, NCH // 2 - 2, 1) as k:
                evacuate(k + 1, 1)
                evacuate(k + 2, 0)
            evacuate(NCH // 2 - 1, 1, prepare=False)

        @block.vector
        def _(dve):
            for m in range(CT):
                for k in range(NCH):
                    if k % (NCH // 2) == 0:
                        dve.wait_ge(x_loaded[m][k // (NCH // 2)], 16)
                    nc.vector.bn_stats(stats[:, m, k, :], x_sb[:, m, k * CH:(k + 1) * CH]).then_inc(stats_done, 1)
            dve.wait_ge(stats_done, CT * NCH)
            gn_vector(dve)

            def normalise(n):
                wait(dve, xn_lo_done, CT * n)
                for m in range(CT):
                    nc.vector.tensor_scalar(xn[:, m, :], x_sb[:, m, bass.ts(n, CH)], mean[:, m:m + 1],
                                            rstd[:, m:m + 1], ALU.subtract, ALU.mult).then_inc(xn_done, 1)

            def normalised_lo(n, slot):
                for m in range(CT):
                    dve.wait_ge(xn_hi_done, CT * n + m + 1)
                    nc.vector.tensor_tensor(xn_lo[:, slot, m, :], xn[:, m, :], xn_hi[:, slot, m, :].bitcast(F32),
                                            ALU.subtract).then_inc(xn_lo_done, 1)

            def evacuate(k, slot, prepare=True):
                n = 2 * k + slot
                for m in range(CT):
                    if m == 0 and prepare:
                        normalise(n + 1)
                    for kind in range(2):
                        dve.wait_ge(qk_hi_done, 8 * n + 2 * m + kind + 1)
                        if kind == 0:
                            dve.wait_ge(sq_done, 2 * (4 * n + m + 1))
                        nc.vector.scalar_tensor_tensor(
                            out=qk_st[:, kind, 1, :], in0=acc[:, (3 * m + kind) % 4, :], scalar=GAIN,
                            in1=qk_st[:, kind, 0, :].bitcast(F32), op0=ALU.mult,
                            op1=ALU.subtract).then_inc(qk_lo_done, 1)
                    if m == 1 and prepare:
                        normalised_lo(n + 1, 1 - slot)
                dve.wait_ge(aa_hi_done, n + 1)
                nc.vector.tensor_tensor(aa_st[:, slot, 1, :], aa_ps[0:HEADS, :],
                                        aa_st[:, slot, 0, :].bitcast(F32), ALU.subtract).then_inc(aa_lo_done, 1)

            normalise(0)
            normalised_lo(0, 0)
            dve.wait_ge(w_hi_done, 3)
            nc.vector.tensor_tensor(w_lo[:, 2, :, :], raw[2], w_hi[:, 2, :, :].bitcast(F32),
                                    ALU.subtract).then_inc(w_lo_done[2], 1)
            normalise(1)
            normalised_lo(1, 1)
            evacuate(0, 0, prepare=False)
            with dve.Fori(0, NCH // 2 - 1, 1) as k:
                evacuate(k, 1)
                evacuate(k + 1, 0)
            evacuate(NCH // 2 - 1, 1, prepare=False)

        @block.gpsimd
        def _(pool):
            def split_squares(n):
                for m in range(CT):
                    pool.wait_ge(sq_done, 2 * (4 * n + m + 1))
                    wait(pool, sq_used, 4 * n + m - 1)
                    nc.gpsimd.tensor_tensor(sq_lo[:, m % 2, :], sq[:, m % 2, :],
                                            sq_hi[:, m % 2, :].bitcast(F32), ALU.subtract).then_inc(sq_lo_done, 1)

            for w in range(2):
                pool.wait_ge(w_hi_done, w + 1)
                nc.gpsimd.tensor_tensor(w_lo[:, w, :, :], raw[w], w_hi[:, w, :, :].bitcast(F32),
                                        ALU.subtract).then_inc(w_lo_done[w], 1)
            split_squares(0)
            with pool.Fori(0, NCH - 1, 1) as k:
                split_squares(k + 1)

        @block.tensor
        def _(pe):
            pe.wait_ge(consts_loaded, 32)
            gn_tensor(pe)

            def group(n, slot, p):
                m, kind = divmod(p, 3)
                if isinstance(n, int) and n == 0:
                    pe.wait_ge(w_lo_done[kind], 1)
                wait_bank(pe, n, p)
                cols = slice(m * P, (m + 1) * P)
                for i in range(3 * CT):
                    c, term = divmod(i, 3)
                    if p == 0 and term == 0:
                        pe.wait_ge(xn_lo_done, CT * n + c + 1)
                    if kind == 2:
                        stationary = (xn_lo if term == 2 else xn_hi)[:, slot, c, cols]
                        moving = (w_lo if term == 1 else w_hi)[:, 2, c, :]
                    else:
                        stationary = (w_lo if term == 2 else w_hi)[:, kind, c, cols]
                        moving = (xn_lo if term == 1 else xn_hi)[:, slot, c, :]
                    last = nc.tensor.matmul(acc[:, p % 4, :], stationary, moving,
                                            start=(i == 0), stop=(i == 3 * CT - 1))
                last.then_inc(v_ready if kind == 2 else qk_ready, 1)

            def chunk(k, slot):
                n = 2 * k + slot
                for m in range(CT):
                    for kind in range(3):
                        group(n, slot, 3 * m + kind)
                    pe.wait_ge(sq_lo_done, 4 * n + m + 1)
                    if m == 0:
                        wait(pe, aa_lo_done, n)
                    nc.tensor.matmul(aa_ps[:, :], sel[:, m, :], sq_hi[:, m % 2, :], start=(m == 0), stop=False)
                    last = nc.tensor.matmul(aa_ps[:, :], sel[:, m, :], sq_lo[:, m % 2, :],
                                            start=False, stop=(m == CT - 1))
                    last.then_inc(sq_used, 1)

            pe.wait_ge(sel_done, 1)
            chunk(0, 0)
            with pe.Fori(0, NCH // 2 - 1, 1) as k:
                chunk(k, 1)
                chunk(k + 1, 0)
            chunk(NCH // 2 - 1, 1)


def attention(nc, ident_d, q_s, k_s, v_s, aa_s, o_s):
    with ExitStack() as ctx:
        def sb(name, shape, dt=F32):
            return ctx.enter_context(nc.sbuf_tensor(name, shape, dt))

        def sem(name):
            return ctx.enter_context(nc.semaphore(name))

        k_max = sb("p2_k_max", [D + 2, 2, N], F32R)
        k_one = sb("p2_k_one", [P, 2, N], F32R)
        k_two = sb("p2_k_two", [D + 3, 2, N], F32R)
        v_sb = sb("p2_v", [P, JT, P])
        q_max = sb("p2_q_max", [D + 2, 2, 2, CH], F32R)
        q_one = sb("p2_q_one", [P, 2, 2, CH], F32R)
        q_two = sb("p2_q_two", [D + 3, 2, 2, CH], F32R)
        probs = sb("p2_probs", [P, PSLOTS, 2, CH])
        row_max = sb("p2_row_max", [P, 2 * CH // P, NCH])
        r_col = sb("p2_r_col", [P, 2 * CH // P])
        r_row = sb("p2_r_row", [2 * CH // P, 2, P], F32R)
        den_dve = sb("p2_den_dve", [P, 2, CH])
        den_pool = sb("p2_den_pool", [P, 2, 2, CH])
        den_sum = sb("p2_den_sum", [P, 2, CH])
        out_raw = sb("p2_out_raw", [P, CH])
        den_inv = sb("p2_den_inv", [P, CH])
        out_norm = sb("p2_out_norm", [P, 2, CH])
        ident = sb("p2_ident", [P, P])
        ones = sb("p2_ones", [P, D])
        scores = ctx.enter_context(nc.psum_tensor("p2_scores", [P, 2, 2, CH], F32))
        max_ps = ctx.enter_context(nc.psum_tensor("p2_max", [P, 2, CH], F32))
        out_ps = ctx.enter_context(nc.psum_tensor("p2_out", [P, CH], F32))
        misc_ps = ctx.enter_context(nc.psum_tensor("p2_misc", [P, CH], F32))

        consts_loaded = sem("p2_consts_loaded")
        q_max_set, q_two_set, k_two_set, ones_set = (
            sem(f"p2_{n}_set") for n in ("q_max", "q_two", "k_two", "ones"))
        km_loaded = [sem(f"p2_km_loaded{c}") for c in range(NCH)]
        kab_loaded = [sem(f"p2_kab_loaded{c}") for c in range(NCH)]
        qm_loaded = [sem(f"p2_qm_loaded{s}") for s in range(2)]
        qab_loaded = [sem(f"p2_qab_loaded{s}") for s in range(2)]
        r_loaded = [sem(f"p2_r_loaded{s}") for s in range(2)]
        max_ready = sem("p2_max_ready")
        max_read = sem("p2_max_read")
        first_max_read = sem("p2_first_max_read")
        r_ready = sem("p2_r_ready")
        r_turned = sem("p2_r_turned")
        r_copied = sem("p2_r_copied")
        scores_ready = sem("p2_scores_ready")
        probs_ready = sem("p2_probs_ready")
        probs_used = sem("p2_probs_used")
        dve_added = sem("p2_dve_added")
        pool_added = sem("p2_pool_added")
        den_summed = sem("p2_den_summed")
        den_ready = sem("p2_den_ready")
        den_inverted = sem("p2_den_inverted")
        out_copied = sem("p2_out_copied")
        normalised = sem("p2_normalised")
        out_stored = [sem(f"p2_out_stored{s}") for s in range(2)]
        block = ctx.enter_context(nc.Block())

        def dve_ops_through(jt):
            return max(DVE_JTS.index(jt), 1)

        def pool_ops_through(jt):
            return max(POOL_JTS.index(jt), 1)

        def units_of(step):
            return range(sum(UNITS_OF_STEPS[:step]), sum(UNITS_OF_STEPS[:step + 1]))

        @block.sync
        def _(sp):
            sp.dma_start(ident[:, :], ident_d).then_inc(consts_loaded, 16)

            def load_k_max(pair, c):
                for h in range(2):
                    cols = slice(c * CH, (c + 1) * CH)
                    sp.dma_start(k_max[0:D, h, cols].bitcast(F32),
                                 k_s[2 * pair + h, 0, :, cols]).then_inc(km_loaded[c], 16)
                    sp.dma_start(k_max[D:D + 2, h, cols].bitcast(F32),
                                 aa_s[2 * pair + h, :, cols]).then_inc(km_loaded[c], 16)

            def load_k_and_v(pair, c):
                cols = slice(c * CH, (c + 1) * CH)
                for h in range(2):
                    head = 2 * pair + h
                    sp.dma_start(k_one[:, h, cols].bitcast(F32),
                                 k_s[head, :, :, cols].rearrange("s c n -> (s c) n")).then_inc(kab_loaded[c], 16)
                    sp.dma_start(k_two[0:D, h, cols].bitcast(F32), k_s[head, 0, :, cols]).then_inc(kab_loaded[c], 16)
                    sp.dma_start(k_two[D:D + 2, h, cols].bitcast(F32),
                                 aa_s[head, :, cols]).then_inc(kab_loaded[c], 16)
                sp.dma_start(v_sb[:, 4 * c:4 * c + 4, :],
                             v_s[pair, :, 4 * c:4 * c + 4, :]).then_inc(kab_loaded[c], 16)

            def load_q_max(pair, chunk, slot):
                for h in range(2):
                    sp.dma_start(q_max[0:D, slot, h, :].bitcast(F32),
                                 q_s[2 * pair + h, 0, :, bass.ts(chunk, CH)]).then_inc(qm_loaded[slot], 16)

            def load_q(pair, chunk, slot):
                for h in range(2):
                    head, cols = 2 * pair + h, bass.ts(chunk, CH)
                    sp.dma_start(q_one[0:D, slot, h, :].bitcast(F32),
                                 q_s[head, 0, :, cols]).then_inc(qab_loaded[slot], 16)
                    sp.dma_start(q_one[D:P, slot, h, :].bitcast(F32),
                                 q_s[head, 0, :, cols]).then_inc(qab_loaded[slot], 16)
                    sp.dma_start(q_two[0:D, slot, h, :].bitcast(F32),
                                 q_s[head, 1, :, cols]).then_inc(qab_loaded[slot], 16)

            load_q_max(0, 0, 0)
            for c in range(NCH):
                load_k_max(0, c)
            load_q(0, 0, 0)
            load_q_max(0, 1, 1)
            sp.wait_ge(k_two_set, 1)
            for c in range(NCH):
                load_k_and_v(0, c)

            def queries_ahead(pair, t, slot, maxima=True):
                tile = NCH * pair + t
                sp.wait_ge(scores_ready, JT * tile + 1)
                if maxima:
                    load_q_max((tile + 2) // NCH, (tile + 2) % NCH, slot)
                load_q((tile + 1) // NCH, (tile + 1) % NCH, 1 - slot)

            def plain_tiles(pair):
                with sp.Fori(0, (NCH - 2) // 2, 1) as k:
                    for slot in range(2):
                        queries_ahead(pair, 2 * k + slot, slot)

            with sp.Fori(0, HEADS // 2 - 1, 1) as pair:
                plain_tiles(pair)
                tile = NCH * pair + NCH - 2
                queries_ahead(pair, NCH - 2, 0)
                for c in range(NCH):
                    sp.wait_ge(max_ready, UNITS * (tile + 1) + 8 * (c + 1))
                    load_k_max(pair + 1, c)
                tile = NCH * pair + NCH - 1
                queries_ahead(pair, NCH - 1, 1)
                for c in range(NCH):
                    sp.wait_ge(scores_ready, JT * tile + 4 * (c + 1))
                    sp.wait_ge(probs_used, JT * tile + 4 * (c + 1))
                    load_k_and_v(pair + 1, c)
            plain_tiles(HEADS // 2 - 1)
            queries_ahead(HEADS // 2 - 1, NCH - 2, 0, maxima=False)

        @block.tensor
        def _(pe):
            pe.wait_ge(consts_loaded, 16)
            pe.wait_ge(ones_set, 1)
            pe.wait_ge(q_max_set, 1)

            def maximum_unit(tile, slot, u, out, start=False):
                c, h, s = u // 8, (u % 8) // 4, u % 4
                if u == 0:
                    pe.wait_ge(qm_loaded[slot], 16 * QM_DMAS * (tile // 2 + 1))
                if u % 8 == 0:
                    pe.wait_ge(km_loaded[c], 16 * KM_DMAS * (tile // NCH + 1))
                if not start:
                    wait(pe, max_read, UNITS * (tile - 1) + u - 1)
                elif u >= 4 and u % 2 == 0:
                    pe.wait_ge(first_max_read, u // 2 - 1)
                nc.tensor.matmul(out, q_max[:, slot, h, s * P:(s + 1) * P],
                                 k_max[:, h, c * CH:(c + 1) * CH], start=True, stop=True).then_inc(max_ready, 1)

            def turn_maxima(tile, first=False):
                pe.wait_ge(r_ready, tile + 1)
                if not first:
                    pe.wait_ge(den_inverted, 2 * (tile - 1))
                nc.tensor.matmul(misc_ps[0:2 * CH // P, 0:P], r_col[:, :], ident[:, :],
                                 start=True, stop=True).then_inc(r_turned, 1)

            def score(tile, slot, jt, h, start):
                if h == 0 and not (start and jt < 2):
                    pe.wait_ge(probs_ready, JT * tile + jt - 1)
                keys = slice(jt * P, (jt + 1) * P)
                nc.tensor.matmul(scores[:, jt % 2, h, :], k_one[:, h, keys], q_one[:, slot, h, :],
                                 start=True, stop=False)
                last = nc.tensor.matmul(scores[:, jt % 2, h, :], k_two[:, h, keys], q_two[:, slot, h, :],
                                        start=False, stop=True)
                if h == 1:
                    last.then_inc(scores_ready, 1)

            def times_v(tile, jt):
                pe.wait_ge(probs_ready, JT * tile + jt + 1)
                for h in range(2):
                    last = nc.tensor.matmul(out_ps[h * D:(h + 1) * D, :], v_sb[:, jt, h * D:(h + 1) * D],
                                            probs[:, jt % PSLOTS, h, :], start=(jt == 0), stop=(jt == JT - 1))
                last.then_inc(probs_used, 1)

            def denominators(tile):
                pe.wait_ge(den_summed, tile + 1)
                pe.wait_ge(r_copied, tile + 2 if tile is not TILES - 1 else TILES)
                for h in range(2):
                    last = nc.tensor.matmul(misc_ps[h * D:(h + 1) * D, :], ones[:, :], den_sum[:, h, :],
                                            start=True, stop=True)
                last.then_inc(den_ready, 1)

            def attend(tile, slot, start=False, maxima=True):
                pe.wait_ge(qab_loaded[slot], 16 * QAB_DMAS * (tile // 2 + 1))
                pe.wait_ge(r_loaded[slot], 32 * (tile // 2 + 1))
                for step in range(STEPS):
                    pe.wait_ge(kab_loaded[step], 16 * KAB_DMAS * (tile // NCH + 1))
                    units = units_of(step) if maxima else ()
                    for i in range(2 * STEP):
                        score(tile, slot, STEP * step + i // 2, i % 2, start)
                        for u in units[:2 * STEP][i:i + 1]:
                            maximum_unit(tile + 1, 1 - slot, u, max_ps[:, u % 2, :])
                        if step == STEPS - 1 and i == 2 * STEP - 2 and maxima:
                            turn_maxima(tile + 1)
                    if step == 0 and not start:
                        for jt in range(JT - STEP, JT):
                            times_v(tile - 1, jt)
                    if step == 1 and not start:
                        pe.wait_ge(out_copied, tile)
                    if step >= 1:
                        for jt in range(STEP * (step - 1), STEP * step):
                            times_v(tile, jt)
                    if step == 2 and not start:
                        denominators(tile - 1)
                    for u in units[2 * STEP:]:
                        maximum_unit(tile + 1, 1 - slot, u, max_ps[:, u % 2, :])

            for u in range(UNITS):
                maximum_unit(0, 0, u, scores[:, u // 2 % 2, u % 2, :], start=True)
            turn_maxima(0, first=True)
            attend(0, 0, start=True)
            attend(1, 1)
            attend(2, 0)
            with pe.Fori(0, (TILES - 4) // 2, 1) as k:
                attend(2 * k + 3, 1)
                attend(2 * k + 4, 0)
            attend(TILES - 1, 1, maxima=False)
            for jt in range(JT - STEP, JT):
                times_v(TILES - 1, jt)
            denominators(TILES - 1)

        @block.scalar
        def _(act):
            def exponentials(tile, jt, start):
                act.wait_ge(scores_ready, JT * tile + jt + 1)
                if not (start and jt < PSLOTS):
                    act.wait_ge(probs_used, JT * tile + jt - PSLOTS + 1)
                    before = tile if jt >= PSLOTS else tile - 1
                    j = (jt - PSLOTS) % JT
                    if j in POOL_JTS:
                        act.wait_ge(pool_added, POOL_OPS * before + pool_ops_through(j))
                    else:
                        act.wait_ge(dve_added, DVE_OPS * before + dve_ops_through(j))
                nc.scalar.activation(probs[:, jt % PSLOTS, :, :], scores[:, jt % 2, :, :], ACT.Exp,
                                     scale=0.25).then_inc(probs_ready, 1)

            def copy_out(tile, first=False):
                act.wait_ge(probs_used, JT * (tile + 1))
                if not first:
                    act.wait_ge(normalised, tile)
                nc.scalar.copy(out_raw[:, :], out_ps[:, :]).then_inc(out_copied, 1)

            def store(tile, slot):
                act.wait_ge(normalised, tile + 1)
                act.dma_start(o_s[tile, :, :], out_norm[:, slot, :]).then_inc(out_stored[slot], 16)

            def load_r(tile, slot):
                act.wait_ge(r_copied, tile + 1)
                for h in range(2):
                    act.dma_start(q_two[D + 2:D + 3, slot, h, :].rearrange("o (s n) -> o s n", n=P).bitcast(F32),
                                  r_row[4 * h:4 * h + 4, slot, :].bitcast(F32)).then_inc(r_loaded[slot], 16)

            def attend(tile, slot, start=False, maxima=True):
                for jt in range(JT):
                    exponentials(tile, jt, start)
                    if jt == JT - 2 and maxima:
                        load_r(tile + 1, 1 - slot)
                    if jt == STEP and not start:
                        copy_out(tile - 1)
                    if jt == JT - 1 and not start:
                        store(tile - 1, 1 - slot)

            act.wait_ge(q_two_set, 1)
            load_r(0, 0)
            attend(0, 0, start=True)
            attend(1, 1)
            attend(2, 0)
            with act.Fori(0, (TILES - 4) // 2, 1) as k:
                attend(2 * k + 3, 1)
                attend(2 * k + 4, 0)
            attend(TILES - 1, 1, maxima=False)
            copy_out(TILES - 1)
            store(TILES - 1, 1)
            for s in range(2):
                act.wait_ge(out_stored[s], 16 * TILES // 2)

        @block.vector
        def _(dve):
            nc.vector.memset(q_max[D:D + 2, :, :, :].bitcast(F32), 1.0).then_inc(q_max_set, 1)
            nc.vector.memset(ones[:, :], 1.0).then_inc(ones_set, 1)

            def maximum_unit(tile, u):
                c, h, s = u // 8, (u % 8) // 4, u % 4
                if u == 0:
                    dve.wait_ge(r_ready, tile)
                dve.wait_ge(max_ready, UNITS * tile + u + 1)
                nc.vector.tensor_reduce(row_max[:, 4 * h + s, c:c + 1], max_ps[:, u % 2, :], AX.X,
                                        ALU.max).then_inc(max_read, 1)

            def row_maxima(tile, first=False):
                if first:
                    dve.wait_ge(first_max_read, UNITS // 2)
                else:
                    dve.wait_ge(max_read, UNITS * tile)
                    dve.wait_ge(r_turned, tile)
                nc.vector.tensor_reduce(r_col[:, :], row_max[:, :, :], AX.X, ALU.max).then_inc(r_ready, 1)

            def copy_maxima(tile, half):
                slot = half[1]
                dve.wait_ge(r_turned, tile + 1)
                dve.wait_ge(r_loaded[slot], 32 * half[0])
                nc.vector.tensor_scalar(r_row[:, slot, :], misc_ps[0:2 * CH // P, 0:P], -1.0, None,
                                        ALU.mult).then_inc(r_copied, 1)

            def add(tile, jt):
                if jt not in DVE_JTS[1:]:
                    return
                k = DVE_JTS.index(jt)
                dve.wait_ge(probs_ready, JT * tile + jt + 1)
                dve.wait_ge(dve_added, DVE_OPS * tile + k - 1)
                before = probs[:, DVE_JTS[0], :, :] if k == 1 else den_dve[:, :, :]
                nc.vector.tensor_tensor(den_dve[:, :, :], before, probs[:, jt % PSLOTS, :, :],
                                        ALU.add).then_inc(dve_added, 1)

            def sum_denominators(tile, slot):
                dve.wait_ge(dve_added, DVE_OPS * (tile + 1))
                dve.wait_ge(pool_added, POOL_OPS * (tile + 1))
                dve.wait_ge(den_ready, tile)
                nc.vector.tensor_tensor(den_sum[:, :, :], den_dve[:, :, :], den_pool[:, slot, :, :],
                                        ALU.add).then_inc(den_summed, 1)
                dve.wait_ge(den_summed, tile + 1)

            def invert(tile, part):
                if part == 0:
                    dve.wait_ge(den_ready, tile + 1)
                    dve.wait_ge(normalised, tile)
                cols = slice(part * CH // 2, (part + 1) * CH // 2)
                nc.vector.reciprocal(den_inv[:, cols], misc_ps[:, cols]).then_inc(den_inverted, 1)

            def normalise(tile, half):
                slot = half[1]
                dve.wait_ge(den_inverted, 2 * (tile + 1))
                dve.wait_ge(out_copied, tile + 1)
                dve.wait_ge(out_stored[slot], 16 * half[0])
                nc.vector.tensor_tensor(out_norm[:, slot, :], out_raw[:, :], den_inv[:, :],
                                        ALU.mult).then_inc(normalised, 1)

            def attend(k, slot, start=False, maxima=True):
                tile = 2 * k + slot
                before = (k, 0) if slot else (k - 1, 1)
                after = (k + 1, 0) if slot else (k, 1)
                for step in range(STEPS):
                    units = units_of(step) if maxima else ()
                    for u in units[:2 * STEP]:
                        maximum_unit(tile + 1, u)
                    if step == STEPS - 1 and maxima:
                        row_maxima(tile + 1)
                        copy_maxima(tile + 1, after)
                    if step == 0 and not start:
                        sum_denominators(tile - 1, 1 - slot)
                    for jt in range(STEP * step, STEP * (step + 1)):
                        add(tile, jt)
                    if step in (3, 4) and not start:
                        invert(tile - 1, step - 3)
                    if step == 5 and not start:
                        normalise(tile - 1, before)
                    for u in units[2 * STEP:]:
                        maximum_unit(tile + 1, u)

            for i in range(UNITS // 2):
                c, column = i // 4, 2 * (i % 4)
                dve.wait_ge(max_ready, 2 * (i + 1))
                nc.vector.tensor_reduce(row_max[:, column:column + 2, c], scores[:, i % 2, :, :], AX.X,
                                        ALU.max).then_inc(first_max_read, 1)
            row_maxima(0, first=True)
            copy_maxima(0, (0, 0))
            attend(0, 0, start=True)
            attend(0, 1)
            attend(1, 0)
            with dve.Fori(0, (TILES - 4) // 2, 1) as k:
                attend(k + 1, 1)
                attend(k + 2, 0)
            attend(TILES // 2 - 1, 1, maxima=False)
            sum_denominators(TILES - 1, 1)
            for part in range(2):
                invert(TILES - 1, part)
            normalise(TILES - 1, (TILES // 2 - 1, 1))

        @block.gpsimd
        def _(pool):
            nc.gpsimd.memset(q_two[D:D + 3, :, :, :].bitcast(F32), 1.0).then_inc(q_two_set, 1)
            nc.gpsimd.memset(k_two[D:D + 3, :, :].bitcast(F32), 1.0).then_inc(k_two_set, 1)

            def add_up(tile, slot, first=False):
                for k, jt in enumerate(POOL_JTS[1:], 1):
                    pool.wait_ge(probs_ready, JT * tile + jt + 1)
                    pool.wait_ge(pool_added, POOL_OPS * tile + k - 1)
                    if k == 1 and not first:
                        pool.wait_ge(den_summed, tile - 1)
                    before = probs[:, POOL_JTS[0], :, :] if k == 1 else den_pool[:, slot, :, :]
                    nc.gpsimd.tensor_tensor(den_pool[:, slot, :, :], before, probs[:, jt % PSLOTS, :, :],
                                            ALU.add).then_inc(pool_added, 1)

            add_up(0, 0, first=True)
            add_up(1, 1, first=True)
            with pool.Fori(0, (TILES - 2) // 2, 1) as k:
                add_up(2 * k + 2, 0)
                add_up(2 * k + 3, 1)


def output_and_convolution(nc, x, wo_t, gmat_d, taps_d, o_s, z):
    with ExitStack() as ctx:
        def sb(name, shape, dt=F32):
            return ctx.enter_context(nc.sbuf_tensor(name, shape, dt))

        def sem(name):
            return ctx.enter_context(nc.semaphore(name))

        y_sb = sb("p3_y", [P, CT, N])
        w_hi = sb("p3_w_hi", [P, CT, C], F32R)
        w_lo = sb("p3_w_lo", [P, CT, C], F32R)
        w_raw = sb("p3_w_raw", [P, CT, C])
        o_raw = sb("p3_o_raw", [P, 2, CT, CH])
        o_hi = sb("p3_o_hi", [P, 2, CT, CH], F32R)
        o_lo = sb("p3_o_lo", [P, 2, CT, CH], F32R)
        x_res = sb("p3_x_res", [P, 2, CT, CH])
        gmat = sb("p3_gmat", [P, P])
        taps = sb("p3_taps", [P, 2, P])
        taps_hi = sb("p3_taps_hi", [P, 2, P], F32R)
        taps_lo = sb("p3_taps_lo", [P, 2, P], F32R)
        near = sb("p3_near", [P, 2, CT, CH], F32R)
        stats = sb("p3_stats", [P, CT, NCH, 6])
        mv = sb("p3_mv", [P, CT, 2])
        ex = sb("p3_ex", [P, CT, 2])
        root = sb("p3_root", [P, CT, 2])
        mean = sb("p3_mean", [P, CT])
        rstd = sb("p3_rstd", [P, CT])
        acc = ctx.enter_context(nc.psum_tensor("p3_acc", [P, CT, CH], F32))
        gn_ps = ctx.enter_context(nc.psum_tensor("p3_gn", [P, CT, 2], F32))
        yn, yn_hi, yn_lo, z_st = o_raw, o_hi, o_lo, x_res

        consts_loaded = sem("p3_consts_loaded")
        w_loaded = [sem(f"p3_w_loaded{c}") for c in range(CT)]
        w_hi_done = sem("p3_w_hi_done")
        w_lo_done = sem("p3_w_lo_done")
        o_first_loaded = [sem(f"p3_o_first_loaded{c}") for c in range(CT)]
        o_loaded = [sem(f"p3_o_loaded{s}") for s in range(2)]
        x_loaded = [sem(f"p3_x_loaded{s}") for s in range(2)]
        o_hi_done = sem("p3_o_hi_done")
        o_lo_done = sem("p3_o_lo_done")
        wo_ready = sem("p3_wo_ready")
        y_done = sem("p3_y_done")
        stats_done = sem("p3_stats_done")
        gn_ready = sem("p3_gn_ready")
        taps_hi_done = sem("p3_taps_hi_done")
        taps_lo_done = sem("p3_taps_lo_done")
        zeros_set = sem("p3_zeros_set")
        near_loaded = [sem(f"p3_near_loaded{s}") for s in range(2)]
        yn_done = sem("p3_yn_done")
        yn_hi_done = sem("p3_yn_hi_done")
        yn_lo_done = sem("p3_yn_lo_done")
        conv_ready = sem("p3_conv_ready")
        z_done = sem("p3_z_done")
        z_stored = [sem(f"p3_z_stored{s}") for s in range(2)]
        gn_vector, gn_tensor, gn_scalar = group_statistics(
            nc, lambda n: sem("p3_" + n), stats, mv, ex, gn_ps, gmat, root, mean, rstd, gn_ready)
        block = ctx.enter_context(nc.Block())

        @block.sync
        def _(sp):
            o_tiles = o_s.rearrange("(q t) p n -> t p q n", t=NCH)

            def load_o(n, slot):
                sp.dma_start(o_raw[:, slot, :, :], o_tiles[n, :, :, :]).then_inc(o_loaded[slot], 16)

            def load_x(n, slot):
                sp.dma_start(x_res[:, slot, :, :],
                             x[:, bass.ts(n, CH)].rearrange("(m p) n -> p m n", p=P)).then_inc(x_loaded[slot], 16)

            for c in range(CT):
                sp.dma_start(w_raw[:, c, :], wo_t[c * P:(c + 1) * P, :]).then_inc(w_loaded[c], 16)
                sp.dma_start(o_raw[:, 0, c, :], o_tiles[0, :, c, :]).then_inc(o_first_loaded[c], 16)
            load_o(1, 1)
            load_x(0, 0)
            load_x(1, 1)
            sp.dma_start(gmat[:, :], gmat_d).then_inc(consts_loaded, 16)
            def load_taps(row, part, first, rows, offset):
                sp.dma_start(taps[row:row + rows, part, :],
                             bass.AP(tensor=taps_d.tensor, offset=P - 1 + first * (C - 1) + offset * P,
                                     ap=[[C - 1, rows], [1, P]])).then_inc(consts_loaded, 16)

            sp.wait_ge(zeros_set, 3)
            load_taps(0, 0, 0, P, 1)
            for half in range(2):
                load_taps(half * P // 2, 1, P - REACH, REACH, 2)
                load_taps(half * P // 2 + REACH, 1, 0, REACH, 0)
            with sp.Fori(0, (NCH - 2) // 2, 1) as k:
                for slot in range(2):
                    sp.wait_ge(o_lo_done, CT * (2 * k + slot + 1))
                    load_o(2 * k + slot + 2, slot)
                    sp.wait_ge(y_done, CT * (2 * k + slot + 1))
                    load_x(2 * k + slot + 2, slot)

            def load_near(n, slot):
                for row, source, done in ((0, yn_hi, yn_hi_done), (P // 2, yn_lo, yn_lo_done)):
                    sp.wait_ge(done, CT * (n + 1))
                    from_before = slice(row, row + REACH)
                    from_after = slice(row + REACH, row + 2 * REACH)
                    for rows, channels, outputs, inputs in (
                            (from_before, slice(P - REACH, P), slice(1, CT), slice(0, CT - 1)),
                            (from_before, slice(P - REACH, P), 0, CT - 1),
                            (from_after, slice(0, REACH), slice(0, CT - 1), slice(1, CT)),
                            (from_after, slice(0, REACH), CT - 1, 0)):
                        sp.dma_start(near[rows, slot, outputs, :].bitcast(F32),
                                     source[channels, slot, inputs, :].bitcast(F32)).then_inc(near_loaded[slot], 16)

            def store(n, slot):
                sp.wait_ge(z_done, CT * (n + 1))
                sp.dma_start(z[:, bass.ts(n, CH)].rearrange("(m p) n -> p m n", p=P),
                             z_st[:, slot, :, :]).then_inc(z_stored[slot], 16)

            load_near(0, 0)
            load_near(1, 1)
            with sp.Fori(0, NCH // 2 - 1, 1) as k:
                store(2 * k, 0)
                load_near(2 * k + 2, 0)
                store(2 * k + 1, 1)
                load_near(2 * k + 3, 1)
            store(NCH - 2, 0)
            for m in range(CT):
                sp.wait_ge(z_done, CT * (NCH - 1) + m + 1)
                sp.dma_start(z[m * P:(m + 1) * P, (NCH - 1) * CH:], z_st[:, 1, m, :]).then_inc(z_stored[1], 16)
            sp.wait_ge(z_stored[0], 16 * NCH // 2)
            sp.wait_ge(z_stored[1], 16 * (NCH // 2 - 1 + CT))

        @block.scalar
        def _(act):
            def split(n, slot, loads=None):
                if loads is not None:
                    act.wait_ge(o_loaded[slot], 16 * loads)
                    wait(act, wo_ready, CT * (n - 1))
                for c in range(CT):
                    if loads is None:
                        act.wait_ge(w_loaded[c], 16)
                        nc.scalar.copy(w_hi[:, c, :], w_raw[:, c, :]).then_inc(w_hi_done, 1)
                        act.wait_ge(o_first_loaded[c], 16)
                    nc.scalar.copy(o_hi[:, slot, c, :], o_raw[:, slot, c, :]).then_inc(o_hi_done, 1)

            split(0, 0)
            split(1, 1, loads=1)
            with act.Fori(0, NCH // 2 - 1, 1) as k:
                split(2 * k + 2, 0, loads=k + 1)
                split(2 * k + 3, 1, loads=k + 2)
            act.wait_ge(consts_loaded, 16 * 6)
            nc.scalar.copy(taps_hi[:, :, :], taps[:, :, :]).then_inc(taps_hi_done, 1)
            gn_scalar(act)

            def normalised_hi(k, slot):
                n = 2 * k + slot
                wait(act, conv_ready, CT * (n - 1))
                if isinstance(n, int) and n < 2:
                    act.wait_ge(wo_ready, CT * NCH)
                for m in range(CT):
                    act.wait_ge(yn_done, CT * n + m + 1)
                    nc.scalar.copy(yn_hi[:, slot, m, :], yn[:, slot, m, :]).then_inc(yn_hi_done, 1)

            normalised_hi(0, 0)
            normalised_hi(0, 1)
            with act.Fori(0, NCH // 2 - 1, 1) as k:
                normalised_hi(k + 1, 0)
                normalised_hi(k + 1, 1)

        @block.vector
        def _(dve):
            def split(n, slot, first=False):
                for c in range(CT):
                    if first:
                        dve.wait_ge(w_hi_done, c + 1)
                        nc.vector.tensor_tensor(w_lo[:, c, :], w_raw[:, c, :], w_hi[:, c, :].bitcast(F32),
                                                ALU.subtract).then_inc(w_lo_done, 1)
                    dve.wait_ge(o_hi_done, CT * n + c + 1)
                    nc.vector.tensor_tensor(o_lo[:, slot, c, :], o_raw[:, slot, c, :],
                                            o_hi[:, slot, c, :].bitcast(F32), ALU.subtract).then_inc(o_lo_done, 1)

            def statistics(n, m):
                dve.wait_ge(y_done, CT * n + m + 1)
                nc.vector.bn_stats(stats[:, m, n, :], y_sb[:, m, bass.ts(n, CH)]).then_inc(stats_done, 1)

            def residual(n, k, slot):
                dve.wait_ge(x_loaded[slot], 16 * (k + 1))
                for m in range(CT):
                    dve.wait_ge(wo_ready, CT * n + m + 1)
                    nc.vector.scalar_tensor_tensor(
                        out=y_sb[:, m, bass.ts(n, CH)], in0=acc[:, m, :], scalar=GAIN,
                        in1=x_res[:, slot, m, :], op0=ALU.mult, op1=ALU.add).then_inc(y_done, 1)
                    if m:
                        statistics(n, m - 1)
                statistics(n, CT - 1)

            split(0, 0, first=True)
            with dve.Fori(0, NCH // 2 - 1, 1) as k:
                split(2 * k + 1, 1)
                residual(2 * k, k, 0)
                split(2 * k + 2, 0)
                residual(2 * k + 1, k, 1)
            split(NCH - 1, 1)
            residual(NCH - 2, NCH // 2 - 1, 0)
            dve.wait_ge(taps_hi_done, 1)
            dve.wait_ge(zeros_set, 3)
            nc.vector.tensor_tensor(taps_lo[:, 0, :], taps[:, 0, :], taps_hi[:, 0, :].bitcast(F32),
                                    ALU.subtract).then_inc(taps_lo_done, 1)
            nc.vector.tensor_tensor(taps_lo[0:P // 2, 1, :], taps[0:P // 2, 1, :],
                                    taps_hi[0:P // 2, 1, :].bitcast(F32), ALU.subtract).then_inc(taps_lo_done, 1)
            residual(NCH - 1, NCH // 2 - 1, 1)
            dve.wait_ge(stats_done, CT * NCH)
            gn_vector(dve)

            def normalise(k, slot):
                n = 2 * k + slot
                wait(dve, yn_lo_done, CT * (n - 1))
                for m in range(CT):
                    nc.vector.tensor_scalar(yn[:, slot, m, :], y_sb[:, m, bass.ts(n, CH)], mean[:, m:m + 1],
                                            rstd[:, m:m + 1], ALU.subtract, ALU.mult).then_inc(yn_done, 1)

            def finish(k, slot):
                wait(dve, z_stored[slot], 16 * k)
                for m in range(CT):
                    dve.wait_ge(conv_ready, CT * (2 * k + slot) + m + 1)
                    nc.vector.tensor_tensor(z_st[:, slot, m, :], acc[:, m, :],
                                            y_sb[:, m, bass.ts(2 * k + slot, CH)], ALU.add).then_inc(z_done, 1)

            normalise(0, 0)
            normalise(0, 1)
            for slot in range(2):
                normalise(1, slot)
                finish(0, slot)
            with dve.Fori(0, NCH // 2 - 2, 1) as k:
                for slot in range(2):
                    normalise(k + 2, slot)
                    finish(k + 1, slot)
            finish(NCH // 2 - 1, 0)
            finish(NCH // 2 - 1, 1)

        @block.gpsimd
        def _(pool):
            nc.gpsimd.memset(taps[:, 1, :], 0.0).then_inc(zeros_set, 1)
            nc.gpsimd.memset(near[:, :, :, :].bitcast(F32), 0.0).then_inc(zeros_set, 1)
            pool.wait_ge(zeros_set, 2)
            nc.gpsimd.memset(taps_lo[P // 2:P, 1, :].bitcast(F32), 0.0).then_inc(zeros_set, 1)
            pool.wait_ge(zeros_set, 3)

            def normalised_lo(n, slot):
                wait(pool, conv_ready, CT * (n - 1))
                if isinstance(n, int):
                    pool.wait_ge(wo_ready, CT * NCH)
                for m in range(CT):
                    pool.wait_ge(yn_hi_done, CT * n + m + 1)
                    nc.gpsimd.tensor_tensor(yn_lo[:, slot, m, :], yn[:, slot, m, :],
                                            yn_hi[:, slot, m, :].bitcast(F32), ALU.subtract).then_inc(yn_lo_done, 1)

            normalised_lo(0, 0)
            normalised_lo(1, 1)
            with pool.Fori(0, NCH // 2 - 1, 1) as k:
                normalised_lo(2 * k + 2, 0)
                normalised_lo(2 * k + 3, 1)

        @block.tensor
        def _(pe):
            def project(k, slot):
                for m in range(CT):
                    wait(pe, y_done, 8 * k + (m + 1 if slot else 0))
                    cols = slice(m * P, (m + 1) * P)
                    for i in range(3 * CT):
                        c, term = divmod(i, 3)
                        if m == 0 and term == 0:
                            if isinstance(k, int) and k + slot == 0:
                                pe.wait_ge(w_lo_done, c + 1)
                            pe.wait_ge(o_lo_done, CT * (2 * k + slot) + c + 1)
                        last = nc.tensor.matmul(acc[:, m, :],
                                                (w_lo if term == 2 else w_hi)[:, c, cols],
                                                (o_lo if term == 1 else o_hi)[:, slot, c, :],
                                                start=(i == 0), stop=(i == 3 * CT - 1))
                    last.then_inc(wo_ready, 1)

            def convolve(k, slot):
                for m in range(CT):
                    wait(pe, z_done, 8 * k + (m + 1 if slot else 0))
                    pe.wait_ge(yn_lo_done, CT * (2 * k + slot) + m + 1)
                    for i, (weight, moving) in enumerate(((taps_hi, yn_hi), (taps_hi, yn_lo), (taps_lo, yn_hi))):
                        nc.tensor.matmul(acc[:, m, :], weight[:, 0, :], moving[:, slot, m, :],
                                         start=(i == 0), stop=False)
                pe.wait_ge(near_loaded[slot], 16 * 8 * (k + 1))
                for m in range(CT):
                    nc.tensor.matmul(acc[:, m, :], taps_hi[:, 1, :], near[:, slot, m, :], start=False, stop=False)
                    nc.tensor.matmul(acc[:, m, :], taps_lo[:, 1, :], near[:, slot, m, :],
                                     start=False, stop=True).then_inc(conv_ready, 1)

            project(0, 0)
            project(0, 1)
            with pe.Fori(0, NCH // 2 - 1, 1) as k:
                project(k + 1, 0)
                project(k + 1, 1)
            pe.wait_ge(consts_loaded, 16 * 6)
            gn_tensor(pe)
            pe.wait_ge(y_done, CT * NCH)
            pe.wait_ge(taps_lo_done, 2)
            convolve(0, 0)
            convolve(0, 1)
            with pe.Fori(0, NCH // 2 - 1, 1) as k:
                convolve(k + 1, 0)
                convolve(k + 1, 1)


def build(nc, x, wq_t, wk_t, wv_t, wo_t, taps, gmat, sel, ident, z):
    q_s = nc.dram_tensor("q_scratch", [HEADS, 2, D, N], F32, kind="Internal").ap()
    k_s = nc.dram_tensor("k_scratch", [HEADS, 2, D, N], F32, kind="Internal").ap()
    v_s = nc.dram_tensor("v_scratch", [HEADS // 2, P, JT, P], F32, kind="Internal").ap()
    aa_s = nc.dram_tensor("aa_scratch", [HEADS, 2, N], F32, kind="Internal").ap()
    o_s = nc.dram_tensor("o_scratch", [TILES, P, CH], F32, kind="Internal").ap()
    projections(nc, x, wq_t, wk_t, wv_t, gmat, sel, q_s, k_s, v_s, aa_s)
    attention(nc, ident, q_s, k_s, v_s, aa_s, o_s)
    output_and_convolution(nc, x, wo_t, gmat, taps, o_s, z)


def kernel(x, L0_conv_wq, L0_conv_wk, L0_conv_wv, L0_conv_wo, L1_conv_inhibition_filter):
    import numpy as np
    import concourse.bacc as bacc
    from concourse.bass_utils import run_bass_kernel_spmd

    left = (C - SCOPE) // 2
    padded = np.pad(np.asarray(L1_conv_inhibition_filter)[0, 0], (left, C - SCOPE - left))
    channel = np.arange(P)
    arrays = {
        "x_in": np.ascontiguousarray(np.asarray(x).reshape(C, N)),
        "wq_t": np.ascontiguousarray(np.asarray(L0_conv_wq).T),
        "wk_t": np.ascontiguousarray(np.asarray(L0_conv_wk).T),
        "wv_t": np.ascontiguousarray(np.asarray(L0_conv_wv).T),
        "wo_t": np.ascontiguousarray(np.asarray(L0_conv_wo).T),
        "taps": np.ascontiguousarray(np.broadcast_to(padded, (P, C))),
        "gmat": (channel[:, None] // 16 == channel[None, :] // 16).astype(np.float32) / 16,
        "sel": np.where(2 * np.arange(CT)[None, :, None] + channel[:, None, None] // D == channel,
                        -0.5, 0.0).astype(np.float32),
        "ident": np.eye(P, dtype=np.float32),
    }
    nc = bacc.Bacc("TRN2", target_bir_lowering=False, num_devices=1)
    args = [nc.dram_tensor(k, a.shape, F32, kind="ExternalInput").ap() for k, a in arrays.items()]
    z = nc.dram_tensor("z_out", (C, N), F32, kind="ExternalOutput").ap()
    build(nc, *args, z)
    r = run_bass_kernel_spmd(nc, [arrays], core_ids=[0])
    return r.results[0]["z_out"].reshape(1, C, 64, 64)
```
